# Optimizing a Trainium2 kernel written in Bass

```python
import numpy as np
import jax
import jax.numpy as jnp

def _softmax(x, axis=-1):
    return jax.nn.softmax(x, axis=axis)

def _gelu(x):
    return jax.nn.gelu(x, approximate=True)

def _silu(x):
    return jax.nn.silu(x)

def _sigmoid(x):
    return jax.nn.sigmoid(x)

def _layernorm(x, axis=-1, eps=1e-05):
    m = jnp.mean(x, axis=axis, keepdims=True)
    v = jnp.var(x, axis=axis, keepdims=True)
    return (x - m) / jnp.sqrt(v + eps)

def _scatter_add(tgt, idx, src, axis=0):
    return tgt.at[idx].add(src)

def _segment_sum(src, seg, n):
    return jax.ops.segment_sum(src, seg, n)
kernel_name = 'mk_adaln_d1_jaxref_r8_b7d60c'

def setup_inputs(seed: int=0):
    np.random.seed(seed)
    _w = jnp.asarray

    def _L0_attn_setup():
        import jax, jax.numpy as jnp
        import numpy as np
        B, T, HID = (1, 256, 256)
        H = 16
        D = HID // H
        EPS = 1e-05

        def _layer_norm(x, eps=1e-05):
            mu = jnp.mean(x, axis=-1, keepdims=True)
            var = jnp.mean((x - mu) ** 2, axis=-1, keepdims=True)
            return (x - mu) * jax.lax.rsqrt(var + eps)

        def _feature_map(x, gamma, beta):
            return _layer_norm(x * gamma + beta)
        key = jax.random.key(seed)
        ks = jax.random.split(key, 8)
        s = HID ** (-0.5)
        return {'hidden_states': jax.random.normal(ks[0], (B, T, HID), jnp.float32), 'Wq': jax.random.normal(ks[1], (HID, HID), jnp.float32) * s, 'Wk': jax.random.normal(ks[2], (HID, HID), jnp.float32) * s, 'Wv': jax.random.normal(ks[3], (HID, HID), jnp.float32) * s, 'Wo': jax.random.normal(ks[4], (HID, HID), jnp.float32) * s, 'gamma': 1.0 + 0.1 * jax.random.normal(ks[5], (D,), jnp.float32), 'beta': 0.1 * jax.random.normal(ks[6], (D,), jnp.float32)}
    _L0_attn_in = _L0_attn_setup()

    def _L0_ffn_setup():
        import jax, jax.numpy as jnp
        import numpy as np
        DIM_IN = 256
        DIM_HIDDEN = 1024
        key = jax.random.key(seed)
        k_x, k_g, k_u, k_d = jax.random.split(key, 4)
        s_in = 1.0 / np.sqrt(DIM_IN)
        s_hid = 1.0 / np.sqrt(DIM_HIDDEN)
        x = jax.random.normal(k_x, (4, 256, DIM_IN), dtype=jnp.float32)
        w_gate = jax.random.uniform(k_g, (DIM_HIDDEN, DIM_IN), jnp.float32, -s_in, s_in)
        w_up = jax.random.uniform(k_u, (DIM_HIDDEN, DIM_IN), jnp.float32, -s_in, s_in)
        w_down = jax.random.uniform(k_d, (DIM_IN, DIM_HIDDEN), jnp.float32, -s_hid, s_hid)
        return {'x': x, 'w_gate': w_gate, 'w_up': w_up, 'w_down': w_down}
    _L0_ffn_in = _L0_ffn_setup()
    _L0_c = _w((lambda *s: np.random.randn(*s).astype(np.float32) * 0.05)(4, 256))
    _L0_wmod = _w((lambda *s: np.random.randn(*s).astype(np.float32) * 0.05)(256, 6 * 256) * 256 ** (-0.5))
    _d = {'L0_attn_hidden_states': _L0_attn_in['hidden_states'], 'L0_attn_Wq': _L0_attn_in['Wq'], 'L0_attn_Wk': _L0_attn_in['Wk'], 'L0_attn_Wv': _L0_attn_in['Wv'], 'L0_attn_Wo': _L0_attn_in['Wo'], 'L0_attn_gamma': _L0_attn_in['gamma'], 'L0_attn_beta': _L0_attn_in['beta'], 'L0_ffn_w_gate': _L0_ffn_in['w_gate'], 'L0_ffn_w_up': _L0_ffn_in['w_up'], 'L0_ffn_w_down': _L0_ffn_in['w_down'], 'L0_c': _L0_c, 'L0_wmod': _L0_wmod}
    _x0 = _d['L0_attn_hidden_states']
    _d['L0_attn_hidden_states'] = jax.random.normal(jax.random.fold_in(jax.random.key(seed), 1), (4, 1024, 256), dtype=_x0.dtype)
    del _x0
    return _d

def reference(L0_attn_hidden_states, L0_attn_Wq, L0_attn_Wk, L0_attn_Wv, L0_attn_Wo, L0_attn_gamma, L0_attn_beta, L0_ffn_w_gate, L0_ffn_w_up, L0_ffn_w_down, L0_c, L0_wmod):

    def _L0_attn_ref(hidden_states, Wq, Wk, Wv, Wo, gamma, beta):
        import jax, jax.numpy as jnp
        import numpy as np
        B, T, HID = (1, 256, 256)
        H = 16
        D = HID // H
        EPS = 1e-05

        def _layer_norm(x, eps=1e-05):
            mu = jnp.mean(x, axis=-1, keepdims=True)
            var = jnp.mean((x - mu) ** 2, axis=-1, keepdims=True)
            return (x - mu) * jax.lax.rsqrt(var + eps)

        def _feature_map(x, gamma, beta):
            return _layer_norm(x * gamma + beta)
        b, t, _ = hidden_states.shape
        q = (hidden_states @ Wq.T).reshape(b, t, H, D)
        k = (hidden_states @ Wk.T).reshape(b, t, H, D)
        v = (hidden_states @ Wv.T).reshape(b, t, H, D)
        q = _feature_map(q, gamma, beta)
        k = _feature_map(k, gamma, beta)
        q = q * D ** (-0.5)
        attn = jnp.einsum('bqhd,bkhd->bhqk', q, k) ** 2
        mask = jnp.tril(jnp.ones((t, t), dtype=bool))
        attn = jnp.where(mask, attn, 0.0)
        o = jnp.einsum('bhqk,bkhd->bqhd', attn, v)
        z = jnp.sum(attn, axis=-1)
        o = o / (jnp.swapaxes(z, 1, 2)[..., None] + EPS)
        o = o.reshape(b, t, H * D)
        return o @ Wo.T

    def _L0_ffn_ref(x, w_gate, w_up, w_down):
        import jax, jax.numpy as jnp
        import numpy as np
        DIM_IN = 256
        DIM_HIDDEN = 1024
        gate = jnp.einsum('bsd,hd->bsh', x, w_gate)
        up = jnp.einsum('bsd,hd->bsh', x, w_up)
        gated = jax.nn.silu(gate) * up
        return jnp.einsum('bsh,dh->bsd', gated, w_down)
    x = L0_attn_hidden_states
    mod = (_silu(L0_c) @ L0_wmod).reshape(L0_c.shape[0], 6, 1, -1)
    sa, ca, ga, sb, cb, gb = (mod[:, 0], mod[:, 1], mod[:, 2], mod[:, 3], mod[:, 4], mod[:, 5])
    ga = (2 * (ga >= 0) - 1) * jnp.maximum(jnp.abs(ga), 0.25)
    gb = (2 * (gb >= 0) - 1) * jnp.maximum(jnp.abs(gb), 0.25)
    h = _layernorm(x, axis=-1) * (1 + ca) + sa
    x = x + ga * _L0_attn_ref(h, L0_attn_Wq, L0_attn_Wk, L0_attn_Wv, L0_attn_Wo, L0_attn_gamma, L0_attn_beta)
    h = _layernorm(x, axis=-1) * (1 + cb) + sb
    x = x + gb * _L0_ffn_ref(h, L0_ffn_w_gate, L0_ffn_w_up, L0_ffn_w_down)
    return x

_drawn_inputs = setup_inputs


def setup_inputs(seed=0):
    import zlib

    import numpy as np

    out = dict(_drawn_inputs(seed))
    spreads = {}
    factors = {}
    for name, (base, spread) in spreads.items():
        noise = np.random.default_rng([zlib.crc32(name.encode()), seed]).standard_normal(out[name].shape)
        drawn = base * np.exp(spread * noise) if base else spread * noise
        out[name] = jnp.asarray(drawn.astype(out[name].dtype))
    for name, factor in factors.items():
        out[name] = (out[name] * factor).astype(out[name].dtype)
    return out
```

```python
import numpy as np

import concourse.bass as bass
from concourse import mybir
from concourse.alu_op_type import AluOpType as ALU

P = 128
BATCH, SEQ, HID = 4, 1024, 256
HEADS, D = 16, 16
FFN = 1024
LN_EPS = 1e-5
ATT_EPS = 1e-5
KT = HID // P
TILES = BATCH * SEQ // P
TPB = SEQ // P
R = D - 1
NF = R * (R + 1) // 2
PARTS = 3
DV = D + 1
PAIRS = HEADS // 2
HALF = HEADS // 2
MT = FFN // P
ST = 4
SUPERS = TILES // ST


def shape_constants():
    helmert = np.zeros((D, D))
    for i in range(R):
        helmert[: i + 1, i] = 1.0
        helmert[i + 1, i] = -(i + 1.0)
        helmert[:, i] /= np.sqrt((i + 1.0) * (i + 2.0))
    block = np.kron(np.eye(P // D), helmert)
    feat = np.zeros((D, P))
    mono = np.zeros((NF, NF))
    m = R
    for i in range(R):
        feat[i, i] = 1.0
        mono[i, i] = 1.0
        for j in range(i + 1, R):
            feat[i, m] = feat[j, m] = 1.0
            mono[m, m], mono[m, i], mono[m, j] = 0.5, -0.5, -0.5
            m += 1
    weight = np.diag([1.0] * R + [2.0] * (NF - R))
    mix = np.zeros((P, P))
    mix[:NF, :NF] = mono.T @ weight @ mono
    zero = np.zeros((D, P))
    uq = np.concatenate([feat, zero, feat, zero] * 2)
    uk = np.zeros((P, 2 * P))
    for e in range(2):
        uk[64 * e:64 * e + D, P * e:P * e + P] = feat
        uk[64 * e + D:64 * e + 2 * D, P * e:P * e + P] = feat
    const32 = np.concatenate([np.eye(P), block, mix], 1).astype(np.float32)
    const16 = np.concatenate([np.eye(P), uq, uk], 1).astype(np.float16)
    return const32, const16


def wait(eng, sem, count):
    if isinstance(count, int) and count <= 0:
        return
    eng.wait_ge(sem, count)


def build(nc, x, w_q, w_k, w_v_t, w_o_t, gamma, beta, w_gate_t, w_up_t, w_down_t, c_t, w_mod, const32, const16, out):
    from contextlib import ExitStack

    F32, F32R = mybir.dt.float32, mybir.dt.float32r
    F16, BF16 = mybir.dt.float16, mybir.dt.bfloat16
    ACT = mybir.ActivationFunctionType
    AX = mybir.AxisListType

    ctx = ExitStack()
    with ctx:
        def sb(name, shape, dt=F32):
            return ctx.enter_context(nc.sbuf_tensor(name, [P] + shape, dt))

        def ps(name, shape, dt=F32):
            return ctx.enter_context(nc.psum_tensor(name, [P] + shape, dt))

        def sem(name):
            return ctx.enter_context(nc.semaphore(name))

        c32 = sb("c32", [3 * P])
        ident, helmert, mix = c32[:, 0:P], c32[:, P:2 * P], c32[:, 2 * P:3 * P]
        c16 = sb("c16", [4 * P], F16)
        ident16, uq, uk = c16[:, 0:P], c16[:, P:2 * P], c16[:, 2 * P:4 * P]
        xs = sb("xs", [TILES, HID])
        stage = sb("stage", [2, 2048])
        wmod = stage[:, :, :].rearrange("p a b -> p (a b)")[:, 0:KT * 6 * HID].rearrange("p (k n) -> p k n", k=KT)
        gam, bet = sb("gam", [1]), sb("bet", [1])
        gu = sb("gu", [P])
        bet_bc = sb("bet_bc", [P])
        silu_c = sb("silu_c", [KT, BATCH])
        modt = sb("modt", [4, KT, TILES])
        gates = sb("gates", [2, BATCH, HID])
        keep = sb("keep", [TILES])
        bias_p = sb("bias_p", [3, P], BF16)
        bias_r = sb("bias_r", [P])
        bias_rows = sb("bias_rows", [2 * HID], BF16)
        bias_sel = sb("bias_sel", [P], BF16)
        wqk_hi, wqk_lo = sb("wqk_hi", [KT, 2 * HID], F32R), sb("wqk_lo", [KT, 2 * HID], F32R)
        wvo_hi, wvo_lo = sb("wvo_hi", [2, KT, HID], F32R), sb("wvo_lo", [2, KT, HID], F32R)
        wf_hi, wf_lo = sb("wf_hi", [3, 2048], F32R), sb("wf_lo", [3, 2048], F32R)

        bn = sb("bn", [6])
        mv, bn_b, mv2 = sb("mv", [2]), sb("bn_b", [6]), sb("mv2", [2])
        tick = sb("tick", [4])
        r1a, r1s, r1y, r1t = sb("r1a", [1]), sb("r1s", [1]), sb("r1y", [1]), sb("r1t", [1])
        xn = sb("xn", [HID])
        hT = sb("hT", [KT, P])
        h_hi, h_lo = sb("h_hi", [KT, P], F32R), sb("h_lo", [KT, P], F32R)
        sq = sb("sq", [2 * HEADS, D])
        ra, rs, ry, rt = sb("ra", [2 * HEADS]), sb("rs", [2 * HEADS]), sb("ry", [2 * HEADS]), sb("rt", [2 * HEADS])
        qn = sb("qn", [2 * HEADS, D])
        q16, k16 = sb("q16", [HEADS, 4, D], F16), sb("k16", [HEADS, 4, D], F16)
        v_raw, v_r1, v_r2 = sb("v_raw", [HEADS, D]), sb("v_r1", [HEADS, D]), sb("v_r2", [HEADS, D])
        vp = sb("vp", [HEADS, PARTS, DV], BF16)
        qT, kT = sb("qT", [PAIRS, P], F16), sb("kT", [PAIRS, P], F16)
        fk, fk_hi, fk_lo = sb("fk", [HEADS, P]), sb("fk_hi", [HEADS, P], F16), sb("fk_lo", [HEADS, P], F16)
        at, at_hi, at_lo = sb("at", [HEADS, P]), sb("at_hi", [HEADS, P], F16), sb("at_lo", [HEADS, P], F16)
        fq = sb("fq", [HEADS, P])
        state, s_new = sb("state", [HEADS, DV]), sb("s_new", [HEADS, DV])
        ms = sb("ms", [HEADS, DV])
        onum, den, rden, o_n = sb("onum", [HEADS, DV]), sb("den", [HEADS]), sb("rden", [HEADS]), sb("o_n", [HEADS, D])
        oT_hi, oT_lo = sb("oT_hi", [KT, P], F32R), sb("oT_lo", [KT, P], F32R)
        yg = sb("yg", [HID])
        st2 = sb("st2", [TILES, 2])
        r2a, r2s, r2y, r2t = sb("r2a", [TILES]), sb("r2s", [TILES]), sb("r2y", [TILES]), sb("r2t", [TILES])
        h2_hi1, h2_lo1 = sb("h2_hi1", [KT, ST * P], F32R), sb("h2_lo1", [KT, ST * P], F32R)
        h2_hi = [wvo_hi[:, :, :, :].rearrange("p i k n -> p i (k n)"), h2_hi1[:, :, :]]
        h2_lo = [wvo_lo[:, :, :, :].rearrange("p i k n -> p i (k n)"), h2_lo1[:, :, :]]
        g_hi, g_lo = wqk_hi, wqk_lo
        w_in = fq[:, :, :].rearrange("p (i k a) n -> p i k (a n)", i=4, k=KT)
        silu_cb = at[:, HALF:HEADS, :].rearrange("p (k b) n -> p k b n", k=KT)
        raw_ffn = [stage[:, 0, :], stage[:, 1, :], fk[:, :, :].rearrange("p h n -> p (h n)")]
        gtmp = [t[:, :, :].rearrange("p h n -> p (h n)") for t in (at, fk)]
        xn2 = at[:, 0:HALF, :].rearrange("p (i k) n -> p i (k n)", i=ST)
        h2 = at[:, HALF:HEADS, :].rearrange("p (k i) n -> p k (i n)", k=KT)
        sg = fq[:, 0:HALF, :].rearrange("p (k i) n -> p k (i n)", k=2)
        g = fq[:, HALF:HEADS, :].rearrange("p (k i) n -> p k (i n)", k=2)
        yb = fk[:, 0:HALF, :].rearrange("p (i k) n -> p i (k n)", i=ST)
        ob = fk[:, HALF:HEADS, :].rearrange("p (i k) n -> p i (k n)", i=ST)

        big = [ps("big0", [1024]), ps("big1", [1024])]
        acc = ps("acc", [2, 512])
        c0, c1 = ps("c0", [512]), ps("c1", [512])
        acc_h = [acc[:, i, 0:HALF * PARTS * DV].rearrange("p (h s d) -> p h s d", h=HALF, s=PARTS) for i in range(2)]
        sd_h = [c[:, 0:HALF * PARTS * DV].rearrange("p (h s d) -> p h s d", h=HALF, s=PARTS) for c in (c0, c1)]

        ld_small, ld_wmod, ld_win, ld_x0, ld_x, ld_ffn = (sem(n) for n in ("ld_small", "ld_wmod", "ld_win", "ld_x0", "ld_x", "ld_ffn"))
        pr = {n: sem("pr_" + n) for n in (
            "gu", "betbc", "siluc", "silucb", "mods", "gates", "wqk", "bias", "modt", "g1", "g2", "gfin", "wqkhi",
            "bp1", "br1", "bp2", "bp3", "rows0", "rows", "sel0", "sel", "vp0", "vp", "wvohi", "wvolo", "wqklo", "keep0", "keep", "gabs", "tick",
            "state0")}
        names = ("bn1", "mv1", "r1a", "r1s", "r1y", "r1t", "r1u", "r1", "xn", "xT", "hT", "h_hi", "h_split", "qk", "v", "sq", "v_raw",
                 "ss", "ra", "rs", "ry0", "rt0", "rt1", "rt2", "ry", "qn", "q_hi", "k_hi", "q_lo", "k_lo", "v1", "vr1", "v2", "vr2", "v3",
                 "qTp", "kTp", "qT", "kT", "fk0p", "fk1p", "fk0", "fk1", "fkh0", "fkh1", "fkl0", "fkl1",
                 "sc0p", "sc1p", "at0", "at1", "am0", "am1", "ath0", "ath1", "atl0", "atl1",
                 "fq0p", "fq1p", "fq0", "fq1", "accp", "sdp", "sd", "s_new", "state", "msp", "ms",
                 "onum", "den", "rden", "o_n", "oTp", "oT_hi", "oT_lo", "y", "yg", "x1", "bn2", "mv2", "st2")
        s = {n: sem("s_" + n) for n in names}
        fb = {n: sem("f_" + n) for n in (
            "wfh", "wfl", "r2a", "r2s", "r2y0", "r2t0", "r2t1", "r2t2", "r2", "xn2", "hTp", "h2", "h2hi", "h2lo",
            "gate", "up", "sg", "g", "ghi", "glo", "down", "yb", "ob", "stored")}

        block = ctx.enter_context(nc.Block())

        @block.sync
        def _(sp):
            sp.dma_start(silu_c[:, :, :], c_t.rearrange("(k p) b -> p k b", p=P)).then_inc(ld_small, 16)
            sp.dma_start(c32[:, :], const32).then_inc(ld_small, 16)
            sp.dma_start(c16[:, :], const16).then_inc(ld_small, 16)
            sp.dma_start(gam[:, :], gamma).then_inc(ld_small, 16)
            sp.dma_start(bet[:, :], beta).then_inc(ld_small, 16)
            sp.dma_start(xs[:, 0:2, :], x[0:2 * P, :].rearrange("(t p) d -> p t d", p=P)).then_inc(ld_x0, 16)
            for i, w in enumerate((w_q, w_k, w_v_t, w_o_t)):
                sp.dma_start(w_in[:, i, :, :], w.rearrange("(k p) n -> p k n", p=P)).then_inc(ld_win, 16)
            sp.dma_start(wmod, w_mod.rearrange("(k p) n -> p k n", p=P)).then_inc(ld_wmod, 16)
            sp.dma_start(xs[:, 2:TPB, :], x[2 * P:TPB * P, :].rearrange("(t p) d -> p t d", p=P)).then_inc(ld_x, 16)
            for b in range(1, BATCH):
                sp.dma_start(xs[:, TPB * b:TPB * (b + 1), :],
                             x[SEQ * b:SEQ * (b + 1), :].rearrange("(t p) d -> p t d", p=P)).then_inc(ld_x, 16)
            sp.wait_ge(pr["mods"], 1)
            sp.wait_ge(pr["gates"], 1)
            for i, (w, k) in enumerate(((w_gate_t, KT), (w_up_t, KT), (w_down_t, MT))):
                if i == 2:
                    sp.wait_ge(s["fkl0"], TILES)
                    sp.wait_ge(s["fkl1"], TILES)
                sp.dma_start(raw_ffn[i].rearrange("p (k n) -> p k n", k=k),
                             w.rearrange("(k p) n -> p k n", p=P)).then_inc(ld_ffn, 16)
            with sp.Fori(0, SUPERS) as t:
                sp.wait_ge(fb["ob"], t + 1)
                sp.dma_start(out[bass.ds(t * ST * P, ST * P), :].rearrange("(t p) d -> p t d", p=P),
                             ob[:, :, :]).then_inc(fb["stored"], 16)
            sp.wait_ge(fb["stored"], 16 * SUPERS)

        def split_product(out_ap, a_hi, a_lo, b_hi, b_lo, ktiles, first=True, last=True):
            mm = None
            for k in range(ktiles):
                for i, (a, b) in enumerate(((a_hi, b_hi), (a_lo, b_hi), (a_hi, b_lo))):
                    mm = nc.tensor.matmul(out_ap, a(k), b(k), start=first and k == 0 and i == 0,
                                          stop=last and k == ktiles - 1 and i == 2, skip_group_check=True)
            return mm

        @block.tensor
        def _(pe):
            pe.wait_ge(ld_small, 80)
            pe.wait_ge(ld_win, 64)
            pe.wait_ge(pr["gu"], 1)
            for qk in range(2):
                for ko in range(KT):
                    for k, c in enumerate((c0, c1)):
                        mm = nc.tensor.matmul(c[:, qk * HID + ko * P:qk * HID + (ko + 1) * P],
                                              w_in[:, qk, ko, k * P:(k + 1) * P], gu[:, :], start=True, stop=True)
            mm.then_inc(pr["wqk"], 1)
            pe.wait_ge(pr["betbc"], 1)
            nc.tensor.matmul(big[0][:, 512:512 + P], bet_bc[:, :], helmert, start=True, stop=True).then_inc(pr["bias"], 1)
            pe.wait_ge(pr["siluc"], 1)
            pe.wait_ge(ld_wmod, 16)
            for j, param in enumerate((1, 0, 4, 3)):
                for k in range(KT):
                    for i in range(KT):
                        o = (j * KT + k) * BATCH
                        mm = nc.tensor.matmul(big[0][:, o:o + BATCH],
                                              wmod[:, i, param * HID + k * P:param * HID + (k + 1) * P], silu_c[:, i, :],
                                              start=i == 0, stop=i == KT - 1)
            mm.then_inc(pr["mods"], 1)
            pe.wait_ge(pr["silucb"], 1)
            for j, param in enumerate((2, 5)):
                for b in range(BATCH):
                    dst = (big[1][:, b * HID:(b + 1) * HID] if j == 0 else
                           acc[:, b // 2, (b % 2) * HID:(b % 2 + 1) * HID])
                    for i in range(KT):
                        mm = nc.tensor.matmul(dst, silu_cb[:, i, b, :], wmod[:, i, param * HID:(param + 1) * HID],
                                              start=i == 0, stop=i == KT - 1)
            mm.then_inc(pr["gates"], 1)
            for n in ("wqkhi", "wqklo", "modt", "gfin", "br1", "wvohi", "wvolo", "rows", "sel"):
                pe.wait_ge(pr[n], 3 if n == "rows" else 1)

            def x_transpose(n):
                pe.wait_ge(s["xn"], n + 1)
                for k in range(KT):
                    mm = nc.tensor.transpose(c1[:, k * P:(k + 1) * P], xn[:, k * P:(k + 1) * P], ident)
                mm.then_inc(s["xT"], 1)

            def project(n):
                pe.wait_ge(s["h_hi"], n + 1)
                pe.wait_ge(s["h_split"], n + 1)
                nc.tensor.matmul(c0[:, :], bias_sel[:, :], bias_rows[:, :], start=True, stop=False, skip_group_check=True)
                split_product(c0[:, :], lambda k: h_hi[:, k, :], lambda k: h_lo[:, k, :],
                              lambda k: wqk_hi[:, k, :], lambda k: wqk_lo[:, k, :], KT, first=False).then_inc(s["qk"], 1)
                split_product(c1[:, 0:HID], lambda k: h_hi[:, k, :], lambda k: h_lo[:, k, :],
                              lambda k: wvo_hi[:, 0, k, :], lambda k: wvo_lo[:, 0, k, :], KT).then_inc(s["v"], 1)

            def o_transpose(n):
                pe.wait_ge(s["o_n"], n + 1)
                for k in range(KT):
                    mm = nc.tensor.transpose(c1[:, k * P:(k + 1) * P],
                                             o_n[:, :, :].rearrange("p h d -> p (h d)")[:, k * P:(k + 1) * P], ident)
                mm.then_inc(s["oTp"], 1)

            def o_project(n):
                pe.wait_ge(s["oT_hi"], n + 1)
                pe.wait_ge(s["oT_lo"], n + 1)
                split_product(c0[:, 0:HID], lambda k: oT_hi[:, k, :], lambda k: oT_lo[:, k, :],
                              lambda k: wvo_hi[:, 1, k, :], lambda k: wvo_lo[:, 1, k, :], KT).then_inc(s["y"], 1)

            def slot(h):
                return (h % 2) * (HALF // 2) + h // 2

            def step(n, front, back):
                pe.wait_ge(s["k_lo"], n + 1)
                pe.wait_ge(s["q_lo"], n + 1)
                wait(pe, s["sd"], n)
                for j in range(PAIRS):
                    mm = nc.tensor.transpose(c0[:, :].bitcast(F16)[:, j * P:(j + 1) * P],
                                             q16[:, :, :, :].rearrange("p h r d -> p (h r d)")[:, j * P:(j + 1) * P], ident16)
                mm.then_inc(s["qTp"], 1)
                for j in range(PAIRS):
                    mm = nc.tensor.transpose(c1[:, :].bitcast(F16)[:, j * P:(j + 1) * P],
                                             k16[:, :, :, :].rearrange("p h r d -> p (h r d)")[:, j * P:(j + 1) * P], ident16)
                mm.then_inc(s["kTp"], 1)
                pe.wait_ge(s["kT"], n + 1)
                for i in range(2):
                    wait(pe, s[f"fq{i}"], n)
                    for j in range(PAIRS // 2):
                        mm = nc.tensor.matmul(big[i][:, j * 2 * P:(j + 1) * 2 * P], kT[:, i * PAIRS // 2 + j, :], uk,
                                              start=True, stop=True)
                    mm.then_inc(s[f"fk{i}p"], 1)
                pe.wait_ge(s["qT"], n + 1)
                pe.wait_ge(s["state"], n + 1)
                nc.tensor.matmul(c0[:, 0:HEADS * DV], mix, state[:, :, :].rearrange("p h d -> p (h d)"),
                                 start=True, stop=True).then_inc(s["msp"], 1)
                if back:
                    o_transpose(n - 1)
                for i in range(2):
                    pe.wait_ge(s[f"fk{i}"], n + 1)
                    for h in range(HALF):
                        j, e = i * PAIRS // 2 + h // 2, 64 * (h % 2)
                        mm = nc.tensor.matmul(big[i][:, slot(h) * P:(slot(h) + 1) * P], kT[e:e + 64, j, :],
                                              qT[e:e + 64, j, :], start=True, stop=True)
                    mm.then_inc(s[f"sc{i}p"], 1)
                pe.wait_ge(s["ms"], n + 1)
                if back:
                    o_project(n - 1)
                if front:
                    x_transpose(n + 1)
                for i in range(2):
                    pe.wait_ge(s[f"at{i}"], n + 1)
                    for e in range(2):
                        mm = nc.tensor.matmul(big[i][:, e * 512:(e + 1) * 512], uq[64 * e:64 * e + 64, :],
                                              qT[64 * e:64 * e + 64, i * PAIRS // 2:(i + 1) * PAIRS // 2, :],
                                              start=True, stop=True)
                    mm.then_inc(s[f"fq{i}p"], 1)
                if front:
                    if back:
                        pe.wait_ge(s["yg"], n)
                    project(n + 1)
                wait(pe, s["onum"], n)
                pe.wait_ge(s["v1"], n + 1)
                pe.wait_ge(s["v2"], n + 1)
                pe.wait_ge(s["v3"], n + 1)
                for i in range(2):
                    pe.wait_ge(s[f"ath{i}"], n + 1)
                    pe.wait_ge(s[f"atl{i}"], n + 1)
                    for h in range(HALF):
                        for part in (at_hi, at_lo):
                            nc.tensor.matmul(acc_h[i][:, h, :, :], part[:, i * HALF + slot(h), :], vp[:, i * HALF + h, :, :],
                                             start=h == 0 and part is at_hi, stop=False, skip_group_check=True)
                for i in range(2):
                    pe.wait_ge(s[f"fq{i}"], n + 1)
                    for h in range(HALF):
                        mm = nc.tensor.matmul(acc_h[i][:, h, 0, :], fq[:, i * HALF + slot(h), :], ms[:, i * HALF + h, :],
                                              start=False, stop=True, skip_group_check=True)
                mm.then_inc(s["accp"], 1)
                if front:
                    pe.wait_ge(s["qn"], n + 2)
                    pe.wait_ge(s["v_raw"], n + 2)
                elif back:
                    pe.wait_ge(s["yg"], n)
                for i in range(2):
                    pe.wait_ge(s[f"fkh{i}"], n + 1)
                    pe.wait_ge(s[f"fkl{i}"], n + 1)
                    for h in range(HALF):
                        for part in (fk_hi, fk_lo):
                            mm = nc.tensor.matmul(sd_h[i][:, h, :, :], part[:, i * HALF + h, :], vp[:, i * HALF + h, :, :],
                                                  start=part is fk_hi, stop=part is fk_lo)
                mm.then_inc(s["sdp"], 1)

            x_transpose(0)
            project(0)
            step(0, True, False)
            with pe.Fori(1, TILES - 1) as n:
                step(n, True, True)
            step(TILES - 1, False, True)
            pe.wait_ge(s["sd"], TILES)
            o_transpose(TILES - 1)
            o_project(TILES - 1)

            wg = [w[:, 0, :].rearrange("p (k n) -> p k n", k=KT) for w in (wf_hi, wf_lo)]
            wu = [w[:, 1, :].rearrange("p (k n) -> p k n", k=KT) for w in (wf_hi, wf_lo)]
            wd = [w[:, 2, :].rearrange("p (m n) -> p m n", m=MT) for w in (wf_hi, wf_lo)]

            def h2_transpose(t):
                pe.wait_ge(fb["xn2"], t + 1)
                for k, c in enumerate((c0, c1)):
                    for i in range(ST):
                        mm = nc.tensor.transpose(c[:, i * P:(i + 1) * P], xn2[:, i, k * P:(k + 1) * P], ident)
                mm.then_inc(fb["hTp"], 1)

            def gate_up(t, m, buf):
                b = big[m % 2]
                if isinstance(t, int) and t == 0:
                    wait(pe, fb["g"], m - 1)
                else:
                    pe.wait_ge(fb["g"], t * MT + m - 1)
                cols = slice(m * P, (m + 1) * P)
                for w, o, done in ((wg, 0, "gate"), (wu, 512, "up")):
                    split_product(b[:, o:o + 512], lambda k: w[0][:, k, cols], lambda k: w[1][:, k, cols],
                                  lambda k: h2_hi[buf][:, k, :], lambda k: h2_lo[buf][:, k, :], KT).then_inc(fb[done], 1)

            def down(t, m):
                pe.wait_ge(fb["ghi"], t * MT + m + 1)
                pe.wait_ge(fb["glo"], t * MT + m + 1)
                if m == 0:
                    wait(pe, fb["yb"], t)
                for i in range(ST):
                    tok = slice(i * P, (i + 1) * P)
                    mm = split_product(acc[:, i // 2, (i % 2) * HID:(i % 2 + 1) * HID],
                                       lambda k: g_hi[:, m % 2, tok], lambda k: g_lo[:, m % 2, tok],
                                       lambda k: wd[0][:, m, :], lambda k: wd[1][:, m, :], 1,
                                       first=m == 0 and i % 2 == 0, last=m == MT - 1)
                if m == MT - 1:
                    mm.then_inc(fb["down"], 1)

            def super_tile(t, buf, first, last):
                pe.wait_ge(fb["h2hi"], t + 1)
                pe.wait_ge(fb["h2lo"], t + 1)
                for m in range(MT):
                    gate_up(t, m, buf)
                    if m > 0:
                        down(t, m - 1)
                    elif not first:
                        down(t - 1, MT - 1)
                    if m == 3 and not last:
                        h2_transpose(t + 1)

            pe.wait_ge(fb["wfh"], 1)
            pe.wait_ge(fb["wfl"], 1)
            h2_transpose(0)
            super_tile(0, 0, True, False)
            with pe.Fori(0, SUPERS // 2 - 1) as u:
                super_tile(u * 2 + 1, 1, False, False)
                super_tile(u * 2 + 2, 0, False, False)
            super_tile(SUPERS - 1, 1, False, True)
            down(SUPERS - 1, MT - 1)

        @block.scalar
        def _(act):
            act.wait_ge(ld_small, 80)
            nc.scalar.activation(silu_c[:, :, :], silu_c[:, :, :], ACT.Silu).then_inc(pr["siluc"], 1)
            act.preload_act_table(ACT.Sqrt)
            act.wait_ge(pr["wqk"], 1)
            for k, c in enumerate((c0, c1)):
                a = nc.scalar.activation(wqk_hi[:, k, :], c[:, :], ACT.Copy)
            a.then_inc(pr["wqkhi"], 1)
            act.wait_ge(ld_win, 64)
            nc.scalar.activation(wvo_hi[:, :, :, :], w_in[:, 2:4, :, :], ACT.Copy).then_inc(pr["wvohi"], 1)

            def front_start(n):
                act.wait_ge(s["r1a"], n + 1)
                nc.scalar.activation(r1s[:, :], r1a[:, :], ACT.Sqrt).then_inc(s["r1s"], 1)

            def modulate(n):
                act.wait_ge(s["xT"], n + 1)
                wait(act, s["h_split"], n)
                for k in range(KT):
                    a = nc.scalar.activation(hT[:, k, :], c1[:, k * P:(k + 1) * P], ACT.Identity,
                                             scale=modt[:, 0, k, bass.ds(n, 1)], bias=modt[:, 1, k, bass.ds(n, 1)])
                a.then_inc(s["hT"], 1)

            def squares(n):
                act.wait_ge(s["qk"], n + 1)
                wait(act, s["ss"], n)
                nc.scalar.activation(sq[:, :, :].rearrange("p h d -> p (h d)"), c0[:, :], ACT.Square).then_inc(s["sq"], 1)
                act.wait_ge(s["v"], n + 1)
                wait(act, s["v1"], n)
                wait(act, s["vr1"], n)
                nc.scalar.activation(v_raw[:, :, :].rearrange("p h d -> p (h d)"), c1[:, 0:HID],
                                     ACT.Copy).then_inc(s["v_raw"], 1)
                act.wait_ge(s["ra"], n + 1)
                nc.scalar.activation(rs[:, :], ra[:, :], ACT.Sqrt).then_inc(s["rs"], 1)

            def o_hi(n):
                act.wait_ge(s["oTp"], n + 1)
                nc.scalar.activation(oT_hi[:, :, :].rearrange("p k n -> p (k n)"), c1[:, 0:HID],
                                     ACT.Copy).then_inc(s["oT_hi"], 1)

            def step(n, front, back):
                if front:
                    front_start(n + 1)
                act.wait_ge(s["kTp"], n + 1)
                nc.scalar.activation(kT[:, :, :].rearrange("p j n -> p (j n)"), c1[:, :].bitcast(F16),
                                     ACT.Copy).then_inc(s["kT"], 1)
                for i in range(2):
                    act.wait_ge(s[f"fk{i}p"], n + 1)
                    wait(act, s[f"fkl{i}"], n)
                    nc.scalar.activation(fk[:, i * HALF:(i + 1) * HALF, :].rearrange("p h n -> p (h n)"), big[i][:, :],
                                         ACT.Square).then_inc(s[f"fk{i}"], 1)
                if back:
                    o_hi(n - 1)
                for i in range(2):
                    act.wait_ge(s[f"sc{i}p"], n + 1)
                    wait(act, s[f"atl{i}"], n)
                    nc.scalar.activation(at[:, i * HALF:(i + 1) * HALF, :].rearrange("p h n -> p (h n)"), big[i][:, :],
                                         ACT.Square).then_inc(s[f"at{i}"], 1)
                if front:
                    modulate(n + 1)
                for i in range(2):
                    act.wait_ge(s[f"fq{i}p"], n + 1)
                    wait(act, s["accp"], n)
                    nc.scalar.activation(fq[:, i * HALF:(i + 1) * HALF, :].rearrange("p h n -> p (h n)"), big[i][:, :],
                                         ACT.Square).then_inc(s[f"fq{i}"], 1)
                if front:
                    squares(n + 1)

            act.wait_ge(pr["g1"], 1)
            for j in range(2):
                src = big[1][:, :] if j == 0 else acc[:, :, :].rearrange("p a n -> p (a n)")
                a = nc.scalar.activation(gtmp[1][:, j * BATCH * HID:(j + 1) * BATCH * HID], src, ACT.Abs)
            a.then_inc(pr["gabs"], 1)
            act.wait_ge(pr["modt"], 4)
            front_start(0)
            modulate(0)
            squares(0)
            step(0, True, False)
            with act.Fori(1, TILES - 1) as n:
                step(n, True, True)
            step(TILES - 1, False, True)
            o_hi(TILES - 1)
            act.wait_ge(ld_ffn, 48)
            for i in range(3):
                a = nc.scalar.activation(wf_hi[:, i, :], raw_ffn[i], ACT.Copy)
            a.then_inc(fb["wfh"], 1)
            act.wait_ge(fb["r2a"], 1)
            nc.scalar.activation(r2s[:, :], r2a[:, :], ACT.Sqrt).then_inc(fb["r2s"], 1)
            act.preload_act_table(ACT.Silu)

            def modulate2(t):
                act.wait_ge(fb["hTp"], t + 1)
                wait(act, fb["h2lo"], t)
                for k, c in enumerate((c0, c1)):
                    a = nc.scalar.activation(h2[:, k, :], c[:, :], ACT.Identity,
                                             scale=modt[:, 2, k, bass.ds(t * ST, 1)], bias=modt[:, 3, k, bass.ds(t * ST, 1)])
                a.then_inc(fb["h2"], 1)

            def super_tile(t, last):
                for m in range(MT):
                    act.wait_ge(fb["gate"], t * MT + m + 1)
                    if isinstance(t, int) and t == 0:
                        wait(act, fb["g"], m - 1)
                    else:
                        act.wait_ge(fb["g"], t * MT + m - 1)
                    nc.scalar.activation(sg[:, m % 2, :], big[m % 2][:, 0:512], ACT.Silu).then_inc(fb["sg"], 1)
                    if m == 3 and not last:
                        modulate2(t + 1)

            modulate2(0)
            super_tile(0, False)
            with act.Fori(0, SUPERS // 2 - 1) as u:
                super_tile(u * 2 + 1, False)
                super_tile(u * 2 + 2, False)
            super_tile(SUPERS - 1, True)

        @block.vector
        def _(dve):
            tt, ts, cp = nc.vector.tensor_tensor, nc.vector.tensor_scalar, nc.vector.tensor_copy
            nc.vector.memset(vp[:, :, :, :], 0.0).then_inc(pr["vp0"], 1)
            nc.vector.memset(bias_rows[:, :], 0.0).then_inc(pr["rows0"], 1)
            nc.vector.memset(bias_sel[:, :], 0.0).then_inc(pr["sel0"], 1)
            nc.vector.memset(keep[:, :], 1.0).then_inc(pr["keep0"], 1)
            nc.vector.memset(state[:, :, :], 0.0).then_inc(s["state"], 1)
            dve.wait_ge(pr["keep0"], 1)
            nc.vector.memset(vp[:, :, 0, D:DV], 1.0).then_inc(pr["vp"], 1)
            for r in range(3):
                a = nc.vector.memset(bias_sel[32 * r:32 * r + 1, :], 1.0)
            a.then_inc(pr["sel"], 1)
            nc.vector.memset(keep[:, TPB - 1:TILES:TPB], 0.0).then_inc(pr["keep"], 1)
            dve.wait_ge(ld_small, 80)
            ts(gu[:, :], helmert, gam[:, 0:1], None, ALU.mult).then_inc(pr["gu"], 1)
            ts(bet_bc[:, :], ident, 0.0, bet[:, 0:1], ALU.mult, ALU.add).then_inc(pr["betbc"], 1)
            dve.wait_ge(pr["siluc"], 1)
            cp(silu_cb[:, :, :, :], silu_c[:, :, :].unsqueeze(3).broadcast_to([P, KT, BATCH, P])).then_inc(pr["silucb"], 1)
            dve.wait_ge(pr["wqkhi"], 1)
            for k, c in enumerate((c0, c1)):
                a = tt(wqk_lo[:, k, :], c[:, :], wqk_hi[:, k, :].bitcast(F32), ALU.subtract)
            a.then_inc(pr["wqklo"], 1)
            dve.wait_ge(pr["wvohi"], 1)
            tt(wvo_lo[:, :, :, :], w_in[:, 2:4, :, :], wvo_hi[:, :, :, :].bitcast(F32), ALU.subtract).then_inc(pr["wvolo"], 1)
            dve.wait_ge(pr["bias"], 1)
            b_full = big[0][:, 512:512 + P]
            cp(bias_p[:, 0, :], b_full).then_inc(pr["bp1"], 1)
            dve.wait_ge(pr["bp1"], 1)
            tt(bias_r[:, :], b_full, bias_p[:, 0, :], ALU.subtract).then_inc(pr["br1"], 1)
            dve.wait_ge(pr["br1"], 1)
            cp(bias_p[:, 1, :], bias_r[:, :]).then_inc(pr["bp2"], 1)
            dve.wait_ge(pr["bp2"], 1)
            tt(bias_p[:, 2, :], bias_r[:, :], bias_p[:, 1, :], ALU.subtract).then_inc(pr["bp3"], 1)
            dve.wait_ge(pr["bp3"], 1)
            for r in range(3):
                cp(bias_rows[32 * r:32 * r + 1, :].rearrange("p (g n) -> p g n", g=4),
                   bias_p[32 * r:32 * r + 1, r, :].unsqueeze(1).broadcast_to([1, 4, P])).then_inc(pr["rows"], 1)
            dve.wait_ge(pr["mods"], 1)
            for j in range(4):
                src = big[0][:, j * KT * BATCH:(j + 1) * KT * BATCH].rearrange("p (k b) -> p k b", k=KT)
                for k in range(KT):
                    a = ts(modt[:, j, k, :].rearrange("p (b t) -> p b t", b=BATCH),
                           src[:, k, :].unsqueeze(2).broadcast_to([P, BATCH, TPB]), 1.0 if j % 2 == 0 else 0.0, None, ALU.add)
                a.then_inc(pr["modt"], 1)
            dve.wait_ge(pr["gates"], 1)
            for j in range(2):
                src = big[1][:, :] if j == 0 else acc[:, :, :].rearrange("p a n -> p (a n)")
                cols = slice(j * BATCH * HID, (j + 1) * BATCH * HID)
                a = ts(gtmp[0][:, cols], src, 0.0, 2.0, ALU.is_ge, ALU.mult)
            a.then_inc(pr["g1"], 1)
            dve.wait_ge(pr["gabs"], 1)
            b = ts(gtmp[1], gtmp[1], 0.25, None, ALU.max)
            b.then_inc(pr["g2"], 1)
            dve.wait_ge(pr["g1"], 1)
            dve.wait_ge(pr["g2"], 1)
            nc.vector.scalar_tensor_tensor(gates[:, :, :, :].rearrange("p j b n -> p (j b n)"), gtmp[0], -1.0,
                                           gtmp[1], ALU.add, ALU.mult).then_inc(pr["gfin"], 1)
            dve.wait_ge(pr["gfin"], 1)
            dve.wait_ge(pr["rows"], 3)

            def layer_norm(n):
                nc.vector.bn_aggr(mv[:, :], bn[:, :]).then_inc(s["mv1"], 1)
                dve.wait_ge(s["mv1"], n + 1)
                ts(r1a[:, :], mv[:, 1:2], LN_EPS, None, ALU.add).then_inc(s["r1a"], 1)
                dve.wait_ge(s["r1s"], n + 1)
                nc.vector.reciprocal(r1y[:, :], r1s[:, :]).then_inc(s["r1y"], 1)
                dve.wait_ge(s["r1y"], n + 1)
                ts(r1t[:, :], r1y[:, :], r1y[:, 0:1], r1a[:, 0:1], ALU.mult, ALU.mult).then_inc(s["r1t"], 1)
                dve.wait_ge(s["r1t"], n + 1)
                ts(r1s[:, :], r1t[:, :], -0.5, 1.5, ALU.mult, ALU.add).then_inc(s["r1u"], 1)
                dve.wait_ge(s["r1u"], n + 1)
                tt(r1t[:, :], r1y[:, :], r1s[:, :], ALU.mult).then_inc(s["r1"], 1)
                dve.wait_ge(s["r1"], n + 1)
                wait(dve, s["xT"], n)
                ts(xn[:, :], xs[:, bass.ds(n, 1), :].rearrange("p a d -> p (a d)"), mv[:, 0:1], r1t[:, 0:1],
                   ALU.subtract, ALU.mult).then_inc(s["xn"], 1)

            def stats1(n):
                nc.vector.bn_stats(bn[:, :], xs[:, bass.ds(n, 1), :].rearrange("p a d -> p (a d)")).then_inc(s["bn1"], 1)

            def split_h(n):
                dve.wait_ge(s["hT"], n + 1)
                wait(dve, s["v"], n)
                cp(h_hi[:, :, :], hT[:, :, :]).then_inc(s["h_hi"], 1)
                dve.wait_ge(s["h_hi"], n + 1)
                tt(h_lo[:, :, :], hT[:, :, :], h_hi[:, :, :].bitcast(F32), ALU.subtract).then_inc(s["h_split"], 1)

            def head_norms(n):
                dve.wait_ge(s["sq"], n + 1)
                nc.vector.tensor_reduce(rt[:, :], sq[:, :, :], axis=AX.X, op=ALU.add).then_inc(s["ss"], 1)
                dve.wait_ge(s["ss"], n + 1)
                ts(ra[:, :], rt[:, :], 1.0 / D, LN_EPS, ALU.mult, ALU.add).then_inc(s["ra"], 1)
                dve.wait_ge(s["rs"], n + 1)
                nc.vector.reciprocal(ry[:, :], rs[:, :]).then_inc(s["ry0"], 1)
                dve.wait_ge(s["ry0"], n + 1)
                tt(rt[:, :], ry[:, :], ry[:, :], ALU.mult).then_inc(s["rt0"], 1)
                dve.wait_ge(s["rt0"], n + 1)
                tt(rs[:, :], rt[:, :], ra[:, :], ALU.mult).then_inc(s["rt1"], 1)
                dve.wait_ge(s["rt1"], n + 1)
                ts(rt[:, :], rs[:, :], -0.5, 1.5, ALU.mult, ALU.add).then_inc(s["rt2"], 1)
                dve.wait_ge(s["rt2"], n + 1)
                tt(rs[:, :], ry[:, :], rt[:, :], ALU.mult).then_inc(s["ry"], 1)
                dve.wait_ge(s["ry"], n + 1)
                wait(dve, s["q_lo"], n)
                wait(dve, s["k_lo"], n)
                tt(qn[:, :, :], c0[:, :].rearrange("p (h d) -> p h d", d=D),
                   rs[:, :].unsqueeze(2).broadcast_to([P, 2 * HEADS, D]), ALU.mult).then_inc(s["qn"], 1)
                dve.wait_ge(s["qn"], n + 1)
                wait(dve, s["qTp"], n)
                wait(dve, s["kTp"], n)
                cp(q16[:, :, 0:2, :], qn[:, 0:HEADS, :].unsqueeze(2).broadcast_to([P, HEADS, 2, D])).then_inc(s["q_hi"], 1)
                cp(k16[:, :, 0:4:2, :], qn[:, HEADS:, :].unsqueeze(2).broadcast_to([P, HEADS, 2, D])).then_inc(s["k_hi"], 1)

            def split_v(n):
                dve.wait_ge(s["v_raw"], n + 1)
                wait(dve, s["sdp"], n)
                cp(vp[:, :, 0, 0:D], v_raw[:, :, :]).then_inc(s["v1"], 1)
                dve.wait_ge(s["v1"], n + 1)
                tt(v_r1[:, :, :], v_raw[:, :, :], vp[:, :, 0, 0:D], ALU.subtract).then_inc(s["vr1"], 1)
                dve.wait_ge(s["vr1"], n + 1)
                cp(vp[:, :, 1, 0:D], v_r1[:, :, :]).then_inc(s["v2"], 1)
                dve.wait_ge(s["v2"], n + 1)
                tt(vp[:, :, 2, 0:D], v_r1[:, :, :], vp[:, :, 1, 0:D], ALU.subtract).then_inc(s["v3"], 1)

            def o_lo(n):
                dve.wait_ge(s["oT_hi"], n + 1)
                tt(oT_lo[:, :, :].rearrange("p k n -> p (k n)"), c1[:, 0:HID],
                   oT_hi[:, :, :].rearrange("p k n -> p (k n)").bitcast(F32), ALU.subtract).then_inc(s["oT_lo"], 1)

            def gate_y(n):
                dve.wait_ge(s["y"], n + 1)
                tt(yg[:, :], c0[:, 0:HID], gates[:, 0, bass.ds(n // TPB, 1), :].rearrange("p a d -> p (a d)"),
                   ALU.mult).then_inc(s["yg"], 1)

            def stats2(n):
                dve.wait_ge(s["x1"], n + 1)
                nc.vector.bn_stats(bn_b[:, :], xs[:, bass.ds(n, 1), :].rearrange("p a d -> p (a d)")).then_inc(s["bn2"], 1)

            def moments2(n):
                nc.vector.bn_aggr(mv2[:, :], bn_b[:, :]).then_inc(s["mv2"], 1)
                dve.wait_ge(s["mv2"], n + 1)
                cp(st2[:, bass.ds(n, 1), :].rearrange("p a d -> p (a d)"), mv2[:, :]).then_inc(s["st2"], 1)

            def step(n, front, back):
                if front:
                    stats1(n + 1)
                    dve.wait_ge(s["bn1"], n + 2)
                dve.wait_ge(s["qTp"], n + 1)
                cp(qT[:, :, :].rearrange("p j n -> p (j n)"), c0[:, :].bitcast(F16)).then_inc(s["qT"], 1)
                if front:
                    layer_norm(n + 1)
                dve.wait_ge(s["msp"], n + 1)
                cp(ms[:, :, :].rearrange("p h d -> p (h d)"), c0[:, 0:HEADS * DV]).then_inc(s["ms"], 1)
                if back:
                    o_lo(n - 1)
                for i in range(2):
                    hs = slice(i * HALF, (i + 1) * HALF)
                    dve.wait_ge(s[f"fk{i}"], n + 1)
                    cp(fk_hi[:, hs, :], fk[:, hs, :]).then_inc(s[f"fkh{i}"], 1)
                    dve.wait_ge(s[f"fkh{i}"], n + 1)
                    tt(fk_lo[:, hs, :], fk[:, hs, :], fk_hi[:, hs, :], ALU.subtract).then_inc(s[f"fkl{i}"], 1)
                if front:
                    split_h(n + 1)
                if back:
                    gate_y(n - 1)
                for i in range(2):
                    hs = slice(i * HALF, (i + 1) * HALF)
                    dve.wait_ge(s[f"am{i}"], n + 1)
                    cp(at_hi[:, hs, :], at[:, hs, :]).then_inc(s[f"ath{i}"], 1)
                    dve.wait_ge(s[f"ath{i}"], n + 1)
                    tt(at_lo[:, hs, :], at[:, hs, :], at_hi[:, hs, :], ALU.subtract).then_inc(s[f"atl{i}"], 1)
                if back:
                    stats2(n - 1)
                if front:
                    head_norms(n + 1)
                if back:
                    dve.wait_ge(s["bn2"], n)
                dve.wait_ge(s["accp"], n + 1)
                for i in range(2):
                    a = nc.vector.tensor_reduce(onum[:, i * HALF:(i + 1) * HALF, :], acc_h[i].rearrange("p h s d -> p h d s"),
                                                axis=AX.X, op=ALU.add)
                a.then_inc(s["onum"], 1)
                dve.wait_ge(s["onum"], n + 1)
                ts(den[:, :], onum[:, :, D], D * ATT_EPS, None, ALU.add).then_inc(s["den"], 1)
                dve.wait_ge(s["den"], n + 1)
                nc.vector.reciprocal(rden[:, :], den[:, :]).then_inc(s["rden"], 1)
                dve.wait_ge(s["rden"], n + 1)
                tt(o_n[:, :, :], onum[:, :, 0:D], rden[:, :].unsqueeze(2).broadcast_to([P, HEADS, D]),
                   ALU.mult).then_inc(s["o_n"], 1)
                if back:
                    moments2(n - 1)
                dve.wait_ge(s["sdp"], n + 1)
                for i in range(2):
                    a = nc.vector.tensor_reduce(s_new[:, i * HALF:(i + 1) * HALF, :], sd_h[i].rearrange("p h s d -> p h d s"),
                                                axis=AX.X, op=ALU.add)
                a.then_inc(s["sd"], 1)
                dve.wait_ge(s["sd"], n + 1)
                dve.wait_ge(s["msp"], n + 1)
                tt(state[:, :, :], state[:, :, :], s_new[:, :, :], ALU.add).then_inc(s["s_new"], 1)
                dve.wait_ge(s["s_new"], n + 1)
                ts(state[:, :, :], state[:, :, :], keep[:, bass.ds(n, 1)], None, ALU.mult).then_inc(s["state"], 1)
                if front:
                    split_v(n + 1)

            dve.wait_ge(pr["vp"], 1)
            dve.wait_ge(ld_x0, 16)
            stats1(0)
            dve.wait_ge(s["bn1"], 1)
            layer_norm(0)
            split_h(0)
            head_norms(0)
            split_v(0)
            step(0, True, False)
            dve.wait_ge(ld_x, 16 * BATCH)
            with dve.Fori(1, TILES - 1) as n:
                step(n, True, True)
            step(TILES - 1, False, True)
            o_lo(TILES - 1)
            gate_y(TILES - 1)
            stats2(TILES - 1)
            dve.wait_ge(s["bn2"], TILES)
            moments2(TILES - 1)

            dve.wait_ge(s["st2"], TILES)
            ts(r2a[:, :], st2[:, :, 1], LN_EPS, None, ALU.add).then_inc(fb["r2a"], 1)
            dve.wait_ge(fb["wfh"], 1)
            for i in range(3):
                a = tt(wf_lo[:, i, :], raw_ffn[i], wf_hi[:, i, :].bitcast(F32), ALU.subtract)
            a.then_inc(fb["wfl"], 1)
            dve.wait_ge(fb["r2s"], 1)
            nc.vector.reciprocal(r2y[:, :], r2s[:, :]).then_inc(fb["r2y0"], 1)
            dve.wait_ge(fb["r2y0"], 1)
            tt(r2t[:, :], r2y[:, :], r2y[:, :], ALU.mult).then_inc(fb["r2t0"], 1)
            dve.wait_ge(fb["r2t0"], 1)
            tt(r2s[:, :], r2t[:, :], r2a[:, :], ALU.mult).then_inc(fb["r2t1"], 1)
            dve.wait_ge(fb["r2t1"], 1)
            ts(r2t[:, :], r2s[:, :], -0.5, 1.5, ALU.mult, ALU.add).then_inc(fb["r2t2"], 1)
            dve.wait_ge(fb["r2t2"], 1)
            tt(r2s[:, :], r2y[:, :], r2t[:, :], ALU.mult).then_inc(fb["r2"], 1)
            dve.wait_ge(fb["r2"], 1)

            def layer_norm2(t):
                wait(dve, fb["hTp"], t)
                for i in range(ST):
                    a = ts(xn2[:, i, :], xs[:, bass.ds(t * ST + i, 1), :].rearrange("p a d -> p (a d)"),
                           st2[:, bass.ds(t * ST + i, 1), 0:1].rearrange("p a d -> p (a d)"),
                           r2s[:, bass.ds(t * ST + i, 1)], ALU.subtract, ALU.mult)
                a.then_inc(fb["xn2"], 1)

            def split_h2(t, buf):
                dve.wait_ge(fb["h2"], t + 1)
                cp(h2_hi[buf], h2[:, :, :]).then_inc(fb["h2hi"], 1)
                dve.wait_ge(fb["h2hi"], t + 1)
                tt(h2_lo[buf], h2[:, :, :], h2_hi[buf].bitcast(F32), ALU.subtract).then_inc(fb["h2lo"], 1)

            def finish(t):
                dve.wait_ge(fb["down"], t + 1)
                wait(dve, fb["ob"], t)
                for i in range(ST):
                    a = tt(yb[:, i, :], acc[:, i // 2, (i % 2) * HID:(i % 2 + 1) * HID],
                           gates[:, 1, bass.ds(t // (TPB // ST), 1), :].rearrange("p a d -> p (a d)"), ALU.mult)
                a.then_inc(fb["yb"], 1)

            def super_tile(t, buf, first, last):
                for m in range(MT):
                    i = m % 2
                    dve.wait_ge(fb["sg"], t * MT + m + 1)
                    dve.wait_ge(fb["up"], t * MT + m + 1)
                    tt(g[:, i, :], big[i][:, 512:1024], sg[:, i, :], ALU.mult).then_inc(fb["g"], 1)
                    dve.wait_ge(fb["g"], t * MT + m + 1)
                    cp(g_hi[:, i, :], g[:, i, :]).then_inc(fb["ghi"], 1)
                    dve.wait_ge(fb["ghi"], t * MT + m + 1)
                    tt(g_lo[:, i, :], g[:, i, :], g_hi[:, i, :].bitcast(F32), ALU.subtract).then_inc(fb["glo"], 1)
                    if m == 0 and not last:
                        layer_norm2(t + 1)
                    if m == 1 and not first:
                        finish(t - 1)
                    if m == 4 and not last:
                        split_h2(t + 1, 1 - buf)

            layer_norm2(0)
            split_h2(0, 0)
            super_tile(0, 0, True, False)
            with dve.Fori(0, SUPERS // 2 - 1) as u:
                super_tile(u * 2 + 1, 1, False, False)
                super_tile(u * 2 + 2, 0, False, False)
            super_tile(SUPERS - 1, 1, False, True)
            finish(SUPERS - 1)

        @block.gpsimd
        def _(pool):
            nc.gpsimd.memset(tick[:, :], 0.0).then_inc(pr["tick"], 1)
            pool.wait_ge(pr["tick"], 1)

            def low_parts(n):
                pool.wait_ge(s["q_hi"], n + 1)
                nc.gpsimd.tensor_tensor(q16[:, :, 2:4, :], qn[:, 0:HEADS, :].unsqueeze(2).broadcast_to([P, HEADS, 2, D]),
                                        q16[:, :, 0:2, :], ALU.subtract).then_inc(s["q_lo"], 1)
                pool.wait_ge(s["k_hi"], n + 1)
                nc.gpsimd.tensor_tensor(k16[:, :, 1:4:2, :], qn[:, HEADS:, :].unsqueeze(2).broadcast_to([P, HEADS, 2, D]),
                                        k16[:, :, 0:4:2, :], ALU.subtract).then_inc(s["k_lo"], 1)

            def mask(n):
                for i in range(2):
                    a = at[:, i * HALF:(i + 1) * HALF, :]
                    pool.wait_ge(s[f"at{i}"], n + 1)
                    nc.gpsimd.tensor_tensor(tick[:, 2 + i:3 + i], tick[:, 0:1], tick[:, 1:2], ALU.add).then_inc(pr["tick"], 1)
                    nc.gpsimd.affine_select(out=a, in_=a, pattern=[[0, HALF], [1, P]], compare_op=ALU.is_ge, fill=0.0,
                                            base=0, channel_multiplier=-1).then_inc(s[f"am{i}"], 1)

            def residual(n):
                pool.wait_ge(s["yg"], n + 1)
                x1 = xs[:, bass.ds(n, 1), :].rearrange("p a d -> p (a d)")
                nc.gpsimd.tensor_tensor(x1, x1, yg[:, :], ALU.add).then_inc(s["x1"], 1)

            def step(n, front, back):
                mask(n)
                if back:
                    residual(n - 1)
                if front:
                    low_parts(n + 1)

            low_parts(0)
            step(0, True, False)
            with pool.Fori(1, TILES - 1) as n:
                step(n, True, True)
            step(TILES - 1, False, True)
            residual(TILES - 1)

            def finish(t):
                pool.wait_ge(fb["yb"], t + 1)
                wait(pool, fb["stored"], t * 16)
                nc.gpsimd.tensor_tensor(ob[:, :, :], xs[:, bass.ds(t * ST, ST), :], yb[:, :, :], ALU.add).then_inc(fb["ob"], 1)

            finish(0)
            with pool.Fori(1, SUPERS) as t:
                finish(t)


def kernel(L0_attn_hidden_states, L0_attn_Wq, L0_attn_Wk, L0_attn_Wv, L0_attn_Wo, L0_attn_gamma, L0_attn_beta,
           L0_ffn_w_gate, L0_ffn_w_up, L0_ffn_w_down, L0_c, L0_wmod):
    import numpy as _np
    import concourse.bacc as _bacc
    from concourse.bass_utils import run_bass_kernel_spmd as _run

    const32, const16 = shape_constants()
    arrays = {
        "in_x": _np.asarray(L0_attn_hidden_states).reshape(BATCH * SEQ, HID),
        "in_wq": _np.asarray(L0_attn_Wq),
        "in_wk": _np.asarray(L0_attn_Wk),
        "in_wv_t": _np.asarray(L0_attn_Wv).T,
        "in_wo_t": _np.asarray(L0_attn_Wo).T,
        "in_gamma": _np.tile(_np.asarray(L0_attn_gamma), P // D).reshape(P, 1),
        "in_beta": _np.tile(_np.asarray(L0_attn_beta), P // D).reshape(P, 1),
        "in_wg_t": _np.asarray(L0_ffn_w_gate).T,
        "in_wu_t": _np.asarray(L0_ffn_w_up).T,
        "in_wd_t": _np.asarray(L0_ffn_w_down).T,
        "in_c_t": _np.asarray(L0_c).T,
        "in_wmod": _np.asarray(L0_wmod),
        "const32": const32,
        "const16": const16,
    }
    arrays = {k: _np.ascontiguousarray(a) for k, a in arrays.items()}
    nc = _bacc.Bacc("TRN2", target_bir_lowering=False, num_devices=1)
    args = [nc.dram_tensor(k, a.shape, mybir.dt.from_np(a.dtype), kind="ExternalInput").ap() for k, a in arrays.items()]
    out = nc.dram_tensor("out", (BATCH * SEQ, HID), mybir.dt.float32, kind="ExternalOutput").ap()
    build(nc, *args, out)
    r = _run(nc, [arrays], core_ids=[0])
    return r.results[0]["out"].reshape(BATCH, SEQ, HID)
```

```python
import numpy as np

import concourse.bass as bass
from concourse import mybir
from concourse.alu_op_type import AluOpType as ALU

P = 128
BATCH, SEQ, HID = 4, 1024, 256
HEADS, D = 16, 16
FFN = 1024
LN_EPS = 1e-5
ATT_EPS = 1e-5
KT = HID // P
TILES = BATCH * SEQ // P
TPB = SEQ // P
R = D - 1
NF = R * (R + 1) // 2
PARTS = 3
DV = D + 1
PAIRS = HEADS // 2
HALF = HEADS // 2
MT = FFN // P
ST = 4
SUPERS = TILES // ST


def shape_constants():
    helmert = np.zeros((D, D))
    for i in range(R):
        helmert[: i + 1, i] = 1.0
        helmert[i + 1, i] = -(i + 1.0)
        helmert[:, i] /= np.sqrt((i + 1.0) * (i + 2.0))
    block = np.kron(np.eye(P // D), helmert)
    feat = np.zeros((D, P))
    mono = np.zeros((NF, NF))
    m = R
    for i in range(R):
        feat[i, i] = 1.0
        mono[i, i] = 1.0
        for j in range(i + 1, R):
            feat[i, m] = feat[j, m] = 1.0
            mono[m, m], mono[m, i], mono[m, j] = 0.5, -0.5, -0.5
            m += 1
    weight = np.diag([1.0] * R + [2.0] * (NF - R))
    mix = np.zeros((P, P))
    mix[:NF, :NF] = mono.T @ weight @ mono
    zero = np.zeros((D, P))
    uq = np.concatenate([feat, zero, feat, zero] * 2)
    uk = np.zeros((P, 2 * P))
    for e in range(2):
        uk[64 * e:64 * e + D, P * e:P * e + P] = feat
        uk[64 * e + D:64 * e + 2 * D, P * e:P * e + P] = feat
    const32 = np.concatenate([np.eye(P), block, mix], 1).astype(np.float32)
    const16 = np.concatenate([np.eye(P), uq, uk], 1).astype(np.float16)
    return const32, const16


def wait(eng, sem, count):
    if isinstance(count, int) and count <= 0:
        return
    eng.wait_ge(sem, count)


def build(nc, x, w_q, w_k, w_v_t, w_o_t, gamma, beta, w_gate_t, w_up_t, w_down_t, c_t, w_mod, const32, const16, out):
    from contextlib import ExitStack

    F32, F32R = mybir.dt.float32, mybir.dt.float32r
    F16, BF16 = mybir.dt.float16, mybir.dt.bfloat16
    ACT = mybir.ActivationFunctionType
    AX = mybir.AxisListType

    ctx = ExitStack()
    with ctx:
        def sb(name, shape, dt=F32):
            return ctx.enter_context(nc.sbuf_tensor(name, [P] + shape, dt))

        def ps(name, shape, dt=F32):
            return ctx.enter_context(nc.psum_tensor(name, [P] + shape, dt))

        def sem(name):
            return ctx.enter_context(nc.semaphore(name))

        c32 = sb("c32", [3 * P])
        ident, helmert, mix = c32[:, 0:P], c32[:, P:2 * P], c32[:, 2 * P:3 * P]
        c16 = sb("c16", [4 * P], F16)
        ident16, uq, uk = c16[:, 0:P], c16[:, P:2 * P], c16[:, 2 * P:4 * P]
        xs = sb("xs", [TILES, HID])
        wmod = sb("wmod", [KT, 6 * HID])
        raw = wmod[:, :, :].rearrange("p k n -> p (k n)")[:, 0:KT * FFN]
        gam, bet = sb("gam", [1]), sb("bet", [1])
        silu_c = sb("silu_c", [KT, BATCH])
        modt = sb("modt", [4, KT, TILES])
        gates = sb("gates", [2, BATCH, HID])
        keep = sb("keep", [TILES])
        bias_p = sb("bias_p", [3, P], BF16)
        bias_r = sb("bias_r", [P])
        bias_rows = sb("bias_rows", [2 * HID], BF16)
        bias_sel = sb("bias_sel", [P], BF16)
        wqk_hi, wqk_lo = sb("wqk_hi", [KT, 2 * HID], F32R), sb("wqk_lo", [KT, 2 * HID], F32R)
        wvo_hi, wvo_lo = sb("wvo_hi", [2, KT, HID], F32R), sb("wvo_lo", [2, KT, HID], F32R)
        wf_hi, wf_lo = sb("wf_hi", [3, 2048], F32R), sb("wf_lo", [3, 2048], F32R)

        tick = sb("tick", [4])
        bn, mean, rstd = sb("bn", [TILES, 6]), sb("mean", [TILES]), sb("rstd", [TILES])
        na, nb, nd = sb("na", [TILES]), sb("nb", [TILES]), sb("nd", [TILES])
        xn = sb("xn", [HID])
        hT = sb("hT", [KT, P])
        h_hi, h_lo = sb("h_hi", [KT, P], F32R), sb("h_lo", [KT, P], F32R)
        sq = sb("sq", [2 * HEADS, D])
        ra, rs, ry, rt = sb("ra", [2 * HEADS]), sb("rs", [2 * HEADS]), sb("ry", [2 * HEADS]), sb("rt", [2 * HEADS])
        qn = sq
        q16, k16 = sb("q16", [HEADS, 4, D], F16), sb("k16", [HEADS, 4, D], F16)
        v_r1 = sb("v_r1", [HEADS, D])
        vp = sb("vp", [2, HEADS, PARTS, DV], BF16)
        qT, kT = sb("qT", [PAIRS, P], F16), sb("kT", [PAIRS, P], F16)
        fk, fk_hi, fk_lo = sb("fk", [HEADS, P]), sb("fk_hi", [HEADS, P], F16), sb("fk_lo", [HEADS, P], F16)
        at, at_hi, at_lo = sb("at", [HEADS, P]), sb("at_hi", [HEADS, P], F16), sb("at_lo", [HEADS, P], F16)
        fq, fq_hi, fq_lo = sb("fq", [HEADS, P]), sb("fq_hi", [HEADS, P], F16), sb("fq_lo", [HEADS, P], F16)
        state = sb("state", [HEADS, DV])
        ms_r, ms = sb("ms_r", [HEADS, DV]), sb("ms", [2, PARTS, HEADS, DV], BF16)
        den, rden, o_n = sb("den", [HEADS]), sb("rden", [HEADS]), sb("o_n", [HEADS, D])
        oT_hi, oT_lo = sb("oT_hi", [KT, P], F32R), sb("oT_lo", [KT, P], F32R)
        yg = sb("yg", [HID])
        h2_hi1, h2_lo1 = sb("h2_hi1", [KT, ST * P], F32R), sb("h2_lo1", [KT, ST * P], F32R)
        h2_hi = [wvo_hi[:, :, :, :].rearrange("p i k n -> p i (k n)"), h2_hi1[:, :, :]]
        h2_lo = [wvo_lo[:, :, :, :].rearrange("p i k n -> p i (k n)"), h2_lo1[:, :, :]]
        g_hi, g_lo = wqk_hi, wqk_lo
        w_in = fq[:, :, :].rearrange("p (i k a) n -> p i k (a n)", i=4, k=KT)
        gu, bet_bc = at[:, 0, :], at[:, 1, :]
        silu_cb = at[:, HALF:HEADS, :].rearrange("p (k b) n -> p k b n", k=KT)
        gtmp = [t[:, :, :].rearrange("p h n -> p (h n)") for t in (at, fk)]
        xn2 = at[:, 0:HALF, :].rearrange("p (i k) n -> p i (k n)", i=ST)
        h2 = at[:, HALF:HEADS, :].rearrange("p (k i) n -> p k (i n)", k=KT)
        sg = fq[:, 0:HALF, :].rearrange("p (k i) n -> p k (i n)", k=2)
        g = fq[:, HALF:HEADS, :].rearrange("p (k i) n -> p k (i n)", k=2)
        yb = fk[:, 0:HALF, :].rearrange("p (i k) n -> p i (k n)", i=ST)
        ob = fk[:, HALF:HEADS, :].rearrange("p (i k) n -> p i (k n)", i=ST)

        big = [ps("big0", [1024]), ps("big1", [1024])]
        acc = ps("acc", [2, 512])
        c0, c1 = ps("c0", [512]), ps("c1", [512])
        c2 = acc[:, 1, :]
        acc_h = acc[:, 0, 0:HEADS * DV].rearrange("p (h d) -> p h d", h=HEADS)
        c2_h = acc[:, 1, 0:HEADS * DV].rearrange("p (h d) -> p h d", h=HEADS)

        ld_small, ld_wmod, ld_win, ld_x, ld_ffn = (sem(n) for n in ("ld_small", "ld_wmod", "ld_win", "ld_x", "ld_ffn"))
        pr = {n: sem("pr_" + n) for n in (
            "gu", "betbc", "siluc", "silucb", "mods", "gates", "wqk", "bias", "modt", "g1", "g2", "gfin", "wqkhi",
            "bp1", "br1", "bp2", "bp3", "rows0", "rows", "sel0", "sel", "vp0", "vp", "wvohi", "wvolo", "wqklo", "keep0", "keep",
            "fkpad", "gabs", "tick", "bn", "root")}
        nr = {n: sem("nr_" + n) for n in ("m", "mean", "d", "d2", "v", "a", "ae", "s", "y", "t", "u", "r")}
        names = ("xn", "xT", "hT", "h_hi", "h_split", "qk", "v", "sq",
                 "ss", "ra", "rs", "ry0", "rt0", "rt1", "ry", "qn", "q_hi", "k_hi", "q_lo", "k_lo", "v1", "vr1", "v2", "v3",
                 "qTp", "kTp", "qT", "kT", "fk0p", "fk1p", "fk0", "fk1", "fkh0", "fkh1", "fkl0", "fkl1",
                 "sc0p", "sc1p", "at0", "at1", "am0", "am1", "ath0", "ath1", "atl0", "atl1",
                 "fq0p", "fq1p", "fq0", "fq1", "fqh0", "fqh1", "fql0", "fql1", "intra0", "intra1", "accp0", "accp1", "sdp", "state",
                 "msp", "ms1", "msr", "ms2", "ms3",
                 "den", "rden", "o_n", "oTp", "oT_hi", "oT_lo", "y", "yg", "x1", "bn2")
        s = {n: sem("s_" + n) for n in names}
        fb = {n: sem("f_" + n) for n in (
            "wfh", "wfl", "xn2", "hTp", "h2", "h2hi", "h2lo",
            "gate", "up", "sg", "g", "ghi", "glo", "down", "yb", "ob", "stored")}

        block = ctx.enter_context(nc.Block())

        @block.sync
        def _(sp):
            sp.dma_start(silu_c[:, :, :], c_t.rearrange("(k p) b -> p k b", p=P)).then_inc(ld_small, 16)
            sp.dma_start(c32[:, :], const32).then_inc(ld_small, 16)
            sp.dma_start(c16[:, :], const16).then_inc(ld_small, 16)
            sp.dma_start(gam[:, :], gamma).then_inc(ld_small, 16)
            sp.dma_start(bet[:, :], beta).then_inc(ld_small, 16)
            for i, w in enumerate((w_q, w_k, w_v_t, w_o_t)):
                sp.dma_start(w_in[:, i, :, :], w.rearrange("(k p) n -> p k n", p=P)).then_inc(ld_win, 16)
            sp.dma_start(wmod[:, :, :], w_mod.rearrange("(k p) n -> p k n", p=P)).then_inc(ld_wmod, 16)
            for b in range(BATCH):
                sp.dma_start(xs[:, TPB * b:TPB * (b + 1), :],
                             x[SEQ * b:SEQ * (b + 1), :].rearrange("(t p) d -> p t d", p=P)).then_inc(ld_x, 16)
            sp.wait_ge(pr["mods"], 1)
            sp.wait_ge(pr["gates"], 1)
            for i, (w, k) in enumerate(((w_gate_t, KT), (w_up_t, KT), (w_down_t, MT))):
                wait(sp, fb["wfl"], i)
                sp.dma_start(raw.rearrange("p (k n) -> p k n", k=k), w.rearrange("(k p) n -> p k n", p=P)).then_inc(ld_ffn, 16)
            with sp.Fori(0, SUPERS) as t:
                sp.wait_ge(fb["ob"], t + 1)
                sp.dma_start(out[bass.ds(t * ST * P, ST * P), :].rearrange("(t p) d -> p t d", p=P),
                             ob[:, :, :]).then_inc(fb["stored"], 16)
            sp.wait_ge(fb["stored"], 16 * SUPERS)

        def split_product(out_ap, a_hi, a_lo, b_hi, b_lo, ktiles, first=True, last=True):
            mm = None
            for k in range(ktiles):
                for i, (a, b) in enumerate(((a_hi, b_hi), (a_lo, b_hi), (a_hi, b_lo))):
                    mm = nc.tensor.matmul(out_ap, a(k), b(k), start=first and k == 0 and i == 0,
                                          stop=last and k == ktiles - 1 and i == 2, skip_group_check=True)
            return mm

        @block.tensor
        def _(pe):
            pe.wait_ge(ld_small, 80)
            pe.wait_ge(ld_win, 64)
            pe.wait_ge(pr["gu"], 1)
            for qk in range(2):
                for ko in range(KT):
                    for k, c in enumerate((c0, c1)):
                        mm = nc.tensor.matmul(c[:, qk * HID + ko * P:qk * HID + (ko + 1) * P],
                                              w_in[:, qk, ko, k * P:(k + 1) * P], gu, start=True, stop=True)
            mm.then_inc(pr["wqk"], 1)
            pe.wait_ge(pr["betbc"], 1)
            nc.tensor.matmul(big[0][:, 512:512 + P], bet_bc, helmert, start=True, stop=True).then_inc(pr["bias"], 1)
            pe.wait_ge(pr["siluc"], 1)
            pe.wait_ge(ld_wmod, 16)
            for j, param in enumerate((1, 0, 4, 3)):
                for k in range(KT):
                    for i in range(KT):
                        o = (j * KT + k) * BATCH
                        mm = nc.tensor.matmul(big[0][:, o:o + BATCH],
                                              wmod[:, i, param * HID + k * P:param * HID + (k + 1) * P], silu_c[:, i, :],
                                              start=i == 0, stop=i == KT - 1)
            mm.then_inc(pr["mods"], 1)
            pe.wait_ge(pr["silucb"], 1)
            for j, param in enumerate((2, 5)):
                for b in range(BATCH):
                    dst = (big[1][:, b * HID:(b + 1) * HID] if j == 0 else
                           acc[:, b // 2, (b % 2) * HID:(b % 2 + 1) * HID])
                    for i in range(KT):
                        mm = nc.tensor.matmul(dst, silu_cb[:, i, b, :], wmod[:, i, param * HID:(param + 1) * HID],
                                              start=i == 0, stop=i == KT - 1)
            mm.then_inc(pr["gates"], 1)
            for n in ("wqkhi", "wqklo", "modt", "gfin", "br1", "wvohi", "wvolo", "rows", "sel"):
                pe.wait_ge(pr[n], 3 if n == "rows" else 1)

            def x_transpose(n):
                pe.wait_ge(s["xn"], n + 1)
                for k in range(KT):
                    mm = nc.tensor.transpose(c0[:, k * P:(k + 1) * P], xn[:, k * P:(k + 1) * P], ident)
                mm.then_inc(s["xT"], 1)

            def project_qk(n):
                pe.wait_ge(s["h_hi"], n + 1)
                pe.wait_ge(s["h_split"], n + 1)
                nc.tensor.matmul(c0[:, :], bias_sel[:, :], bias_rows[:, :], start=True, stop=False, skip_group_check=True)
                split_product(c0[:, :], lambda k: h_hi[:, k, :], lambda k: h_lo[:, k, :],
                              lambda k: wqk_hi[:, k, :], lambda k: wqk_lo[:, k, :], KT, first=False).then_inc(s["qk"], 1)

            def project_v(n):
                pe.wait_ge(s["state"], n + 1)
                split_product(c2[:, 0:HID], lambda k: h_hi[:, k, :], lambda k: h_lo[:, k, :],
                              lambda k: wvo_hi[:, 0, k, :], lambda k: wvo_lo[:, 0, k, :], KT).then_inc(s["v"], 1)

            def by_parts(out_ap, hi, lo, parts, start, stop):
                for i, (a, p) in enumerate(((hi, 0), (hi, 1), (hi, 2), (lo, 0), (lo, 1))):
                    mm = nc.tensor.matmul(out_ap, a, parts(p), start=start and i == 0, stop=stop and i == 4,
                                          skip_group_check=True)
                return mm

            def o_transpose(n):
                pe.wait_ge(s["o_n"], n + 1)
                for k in range(KT):
                    mm = nc.tensor.transpose(acc[:, 0, k * P:(k + 1) * P],
                                             o_n[:, :, :].rearrange("p h d -> p (h d)")[:, k * P:(k + 1) * P], ident)
                mm.then_inc(s["oTp"], 1)

            def o_project(n):
                pe.wait_ge(s["oT_hi"], n + 1)
                pe.wait_ge(s["oT_lo"], n + 1)
                split_product(c1[:, 0:HID], lambda k: oT_hi[:, k, :], lambda k: oT_lo[:, k, :],
                              lambda k: wvo_hi[:, 1, k, :], lambda k: wvo_lo[:, 1, k, :], KT).then_inc(s["y"], 1)

            def slot(h):
                return (h % 2) * (HALF // 2) + h // 2

            def inside(n, b, i):
                pe.wait_ge(s["v3"], n + 1)
                pe.wait_ge(s[f"ath{i}"], n + 1)
                pe.wait_ge(s[f"atl{i}"], n + 1)
                for h in range(HALF):
                    a, c = i * HALF + slot(h), i * HALF + h
                    mm = by_parts(acc_h[:, c, :], at_hi[:, a, :], at_lo[:, a, :], lambda p: vp[:, b, c, p, :],
                                  c == 0, False)
                mm.then_inc(s[f"intra{i}"], 1)

            def before(n, b, i):
                pe.wait_ge(s["ms3"], n + 1)
                pe.wait_ge(s[f"fqh{i}"], n + 1)
                pe.wait_ge(s[f"fql{i}"], n + 1)
                for h in range(HALF):
                    a, c = i * HALF + slot(h), i * HALF + h
                    mm = by_parts(acc_h[:, c, :], fq_hi[:, a, :], fq_lo[:, a, :], lambda p: ms[:, b, p, c, :], False, True)
                mm.then_inc(s[f"accp{i}"], 1)

            def state_part(n, b):
                pe.wait_ge(s["v3"], n + 1)
                pe.wait_ge(s["msr"], n + 1)
                for i in range(2):
                    pe.wait_ge(s[f"fkh{i}"], n + 1)
                    pe.wait_ge(s[f"fkl{i}"], n + 1)
                    for h in range(i * HALF, (i + 1) * HALF):
                        mm = by_parts(c2_h[:, h, :], fk_hi[:, h, :], fk_lo[:, h, :], lambda p: vp[:, b, h, p, :], True, True)
                mm.then_inc(s["sdp"], 1)

            def key_features(n, i):
                wait(pe, s[f"fqh{i}"], n)
                for j in range(PAIRS // 2):
                    mm = nc.tensor.matmul(big[i][:, j * 2 * P:(j + 1) * 2 * P], kT[:, i * PAIRS // 2 + j, :], uk,
                                          start=True, stop=True)
                mm.then_inc(s[f"fk{i}p"], 1)

            def scores(n, i):
                pe.wait_ge(s[f"fkh{i}"], n + 1)
                for h in range(HALF):
                    j, e = i * PAIRS // 2 + h // 2, 64 * (h % 2)
                    mm = nc.tensor.matmul(big[i][:, slot(h) * P:(slot(h) + 1) * P], kT[e:e + 64, j, :],
                                          qT[e:e + 64, j, :], start=True, stop=True)
                mm.then_inc(s[f"sc{i}p"], 1)

            def query_features(n, i):
                pe.wait_ge(s[f"at{i}"], n + 1)
                for e in range(2):
                    mm = nc.tensor.matmul(big[i][:, e * 512:(e + 1) * 512], uq[64 * e:64 * e + 64, :],
                                          qT[64 * e:64 * e + 64, i * PAIRS // 2:(i + 1) * PAIRS // 2, :],
                                          start=True, stop=True)
                mm.then_inc(s[f"fq{i}p"], 1)

            def step(n, b, front, back, back2):
                wait(pe, s["yg"], n - 2)
                for c, x16, part, done in ((c0, q16, "q_lo", "qTp"), (c1, k16, "k_lo", "kTp")):
                    pe.wait_ge(s[part], n + 1)
                    for j in range(PAIRS):
                        mm = nc.tensor.transpose(c[:, :].bitcast(F16)[:, j * P:(j + 1) * P],
                                                 x16[:, :, :, :].rearrange("p h r d -> p (h r d)")[:, j * P:(j + 1) * P],
                                                 ident16)
                    mm.then_inc(s[done], 1)
                if back2:
                    o_transpose(n - 2)
                project_v(n)
                pe.wait_ge(s["kT"], n + 1)
                key_features(n, 0)
                pe.wait_ge(s["qT"], n + 1)
                if front:
                    x_transpose(n + 1)
                if back:
                    wait(pe, s["oT_lo"], n - 1)
                    inside(n - 1, 1 - b, 0)
                key_features(n, 1)
                if back2:
                    o_project(n - 2)
                if front:
                    project_qk(n + 1)
                if back:
                    inside(n - 1, 1 - b, 1)
                scores(n, 0)
                pe.wait_ge(s["vr1"], n + 1)
                nc.tensor.matmul(c2[:, 0:HEADS * DV], mix, state[:, :, :].rearrange("p h d -> p (h d)"),
                                 start=True, stop=True).then_inc(s["msp"], 1)
                scores(n, 1)
                if back:
                    before(n - 1, 1 - b, 0)
                query_features(n, 0)
                if back:
                    before(n - 1, 1 - b, 1)
                query_features(n, 1)
                if front:
                    state_part(n, b)

            x_transpose(0)
            project_qk(0)
            for n in range(4):
                step(n, n % 2, True, n > 0, n > 1)
            with pe.Fori(2, TILES // 2 - 1) as u:
                step(u * 2, 0, True, True, True)
                step(u * 2 + 1, 1, True, True, True)
            step(TILES - 2, 0, True, True, True)
            step(TILES - 1, 1, False, True, True)
            o_transpose(TILES - 2)
            o_project(TILES - 2)
            pe.wait_ge(s["oT_lo"], TILES - 1)
            for i in range(2):
                inside(TILES - 1, 1, i)
                before(TILES - 1, 1, i)
            o_transpose(TILES - 1)
            pe.wait_ge(s["yg"], TILES - 1)
            o_project(TILES - 1)

            wg = [w[:, 0, :].rearrange("p (k n) -> p k n", k=KT) for w in (wf_hi, wf_lo)]
            wu = [w[:, 1, :].rearrange("p (k n) -> p k n", k=KT) for w in (wf_hi, wf_lo)]
            wd = [w[:, 2, :].rearrange("p (m n) -> p m n", m=MT) for w in (wf_hi, wf_lo)]

            def h2_transpose(t):
                pe.wait_ge(fb["xn2"], t + 1)
                for k, c in enumerate((c0, c1)):
                    for i in range(ST):
                        mm = nc.tensor.transpose(c[:, i * P:(i + 1) * P], xn2[:, i, k * P:(k + 1) * P], ident)
                mm.then_inc(fb["hTp"], 1)

            def gate_up(t, m, buf):
                b = big[m % 2]
                if isinstance(t, int) and t == 0:
                    wait(pe, fb["g"], m - 1)
                else:
                    pe.wait_ge(fb["g"], t * MT + m - 1)
                cols = slice(m * P, (m + 1) * P)
                for w, o, done in ((wg, 0, "gate"), (wu, 512, "up")):
                    split_product(b[:, o:o + 512], lambda k: w[0][:, k, cols], lambda k: w[1][:, k, cols],
                                  lambda k: h2_hi[buf][:, k, :], lambda k: h2_lo[buf][:, k, :], KT).then_inc(fb[done], 1)

            def down(t, m):
                pe.wait_ge(fb["ghi"], t * MT + m + 1)
                pe.wait_ge(fb["glo"], t * MT + m + 1)
                if m == 0:
                    wait(pe, fb["yb"], t)
                for i in range(ST):
                    tok = slice(i * P, (i + 1) * P)
                    mm = split_product(acc[:, i // 2, (i % 2) * HID:(i % 2 + 1) * HID],
                                       lambda k: g_hi[:, m % 2, tok], lambda k: g_lo[:, m % 2, tok],
                                       lambda k: wd[0][:, m, :], lambda k: wd[1][:, m, :], 1,
                                       first=m == 0 and i % 2 == 0, last=m == MT - 1)
                if m == MT - 1:
                    mm.then_inc(fb["down"], 1)

            def super_tile(t, buf, first, last):
                pe.wait_ge(fb["h2hi"], t + 1)
                pe.wait_ge(fb["h2lo"], t + 1)
                for m in range(MT):
                    gate_up(t, m, buf)
                    if m > 0:
                        down(t, m - 1)
                    elif not first:
                        down(t - 1, MT - 1)
                    if m == 3 and not last:
                        h2_transpose(t + 1)

            pe.wait_ge(fb["wfh"], 3)
            pe.wait_ge(fb["wfl"], 3)
            h2_transpose(0)
            super_tile(0, 0, True, False)
            with pe.Fori(0, SUPERS // 2 - 1) as u:
                super_tile(u * 2 + 1, 1, False, False)
                super_tile(u * 2 + 2, 0, False, False)
            super_tile(SUPERS - 1, 1, False, True)
            down(SUPERS - 1, MT - 1)

        @block.scalar
        def _(act):
            act.wait_ge(ld_small, 80)
            nc.scalar.activation(silu_c[:, :, :], silu_c[:, :, :], ACT.Silu).then_inc(pr["siluc"], 1)
            act.preload_act_table(ACT.Sqrt)
            act.wait_ge(pr["wqk"], 1)
            for k, c in enumerate((c0, c1)):
                a = nc.scalar.activation(wqk_hi[:, k, :], c[:, :], ACT.Copy)
            a.then_inc(pr["wqkhi"], 1)
            act.wait_ge(ld_win, 64)
            nc.scalar.activation(wvo_hi[:, :, :, :], w_in[:, 2:4, :, :], ACT.Copy).then_inc(pr["wvohi"], 1)

            def modulate(n):
                act.wait_ge(s["xT"], n + 1)
                wait(act, s["h_split"], n)
                for k in range(KT):
                    a = nc.scalar.activation(hT[:, k, :], c0[:, k * P:(k + 1) * P], ACT.Identity,
                                             scale=modt[:, 0, k, bass.ds(n, 1)], bias=modt[:, 1, k, bass.ds(n, 1)])
                a.then_inc(s["hT"], 1)

            def head_squares(n):
                act.wait_ge(s["qk"], n + 1)
                wait(act, s["q_lo"], n)
                wait(act, s["k_lo"], n)
                nc.scalar.activation(sq[:, :, :].rearrange("p h d -> p (h d)"), c0[:, :], ACT.Square).then_inc(s["sq"], 1)

            def head_roots(n):
                act.wait_ge(s["ra"], n + 1)
                wait(act, s["ry0"], n)
                nc.scalar.activation(rs[:, :], ra[:, :], ACT.Sqrt).then_inc(s["rs"], 1)

            def o_hi(n):
                act.wait_ge(s["oTp"], n + 1)
                wait(act, s["y"], n)
                nc.scalar.activation(oT_hi[:, :, :].rearrange("p k n -> p (k n)"), acc[:, 0, 0:HID],
                                     ACT.Copy).then_inc(s["oT_hi"], 1)

            def flat(t, i, w=P):
                return t[:, i * HALF:(i + 1) * HALF, 0:w]

            def key_features(n, i):
                src = big[i][:, :].rearrange("p (h n) -> p h n", h=HALF)[:, :, 0:NF]
                act.wait_ge(s[f"fk{i}p"], n + 1)
                wait(act, s[f"fkl{i}"], n)
                nc.scalar.activation(flat(fk, i, NF), src, ACT.Square).then_inc(s[f"fk{i}"], 1)
                wait(act, s["sdp"], n)
                nc.scalar.activation(flat(fk_hi, i, NF), src, ACT.Square).then_inc(s[f"fkh{i}"], 1)

            def query_features(n, i):
                src = big[i][:, :].rearrange("p (h n) -> p h n", h=HALF)
                act.wait_ge(s[f"fq{i}p"], n + 1)
                wait(act, s[f"fql{i}"], n)
                nc.scalar.activation(flat(fq, i), src, ACT.Square).then_inc(s[f"fq{i}"], 1)
                wait(act, s[f"accp{i}"], n)
                nc.scalar.activation(flat(fq_hi, i), src, ACT.Square).then_inc(s[f"fqh{i}"], 1)

            def weights(n, i):
                act.wait_ge(s[f"sc{i}p"], n + 1)
                wait(act, s[f"atl{i}"], n)
                nc.scalar.activation(flat(at, i), big[i][:, :].rearrange("p (h n) -> p h n", h=HALF),
                                     ACT.Square).then_inc(s[f"at{i}"], 1)

            def weights_hi(n, i):
                act.wait_ge(s[f"am{i}"], n + 1)
                wait(act, s[f"intra{i}"], n)
                nc.scalar.activation(flat(at_hi, i), flat(at, i), ACT.Copy).then_inc(s[f"ath{i}"], 1)

            def step(n, b, front, back, back2):
                act.wait_ge(s["kTp"], n + 1)
                nc.scalar.activation(kT[:, :, :].rearrange("p j n -> p (j n)"), c1[:, :].bitcast(F16),
                                     ACT.Copy).then_inc(s["kT"], 1)
                if back2:
                    o_hi(n - 2)
                act.wait_ge(s["v"], n + 1)
                wait(act, s["intra1"], n - 1)
                wait(act, s["sdp"], n - 1)
                nc.scalar.activation(vp[:, b, :, 0, 0:D], c2[:, 0:HID].rearrange("p (h d) -> p h d", d=D),
                                     ACT.Copy).then_inc(s["v1"], 1)
                if front:
                    modulate(n + 1)
                key_features(n, 0)
                key_features(n, 1)
                if front:
                    head_squares(n + 1)
                weights(n, 0)
                if front:
                    head_roots(n + 1)
                weights(n, 1)
                query_features(n, 0)
                query_features(n, 1)
                weights_hi(n, 0)
                weights_hi(n, 1)

            act.wait_ge(pr["gates"], 1)
            act.wait_ge(pr["silucb"], 1)
            for j in range(2):
                src = big[1][:, :] if j == 0 else acc[:, :, :].rearrange("p a n -> p (a n)")
                a = nc.scalar.activation(gtmp[1][:, j * BATCH * HID:(j + 1) * BATCH * HID], src, ACT.Abs)
            a.then_inc(pr["gabs"], 1)
            act.wait_ge(pr["modt"], 4)
            act.wait_ge(nr["ae"], 1)
            nc.scalar.activation(nb[:, :], na[:, :], ACT.Sqrt).then_inc(nr["s"], 1)
            modulate(0)
            head_squares(0)
            head_roots(0)
            for n in range(4):
                step(n, n % 2, True, n > 0, n > 1)
                if n < 3:
                    act.wait_ge(ld_ffn, 16 * (n + 1))
                    nc.scalar.activation(wf_hi[:, n, :], raw, ACT.Copy).then_inc(fb["wfh"], 1)
            with act.Fori(2, TILES // 2 - 1) as u:
                step(u * 2, 0, True, True, True)
                step(u * 2 + 1, 1, True, True, True)
            step(TILES - 2, 0, True, True, True)
            step(TILES - 1, 1, False, True, True)
            o_hi(TILES - 2)
            o_hi(TILES - 1)
            act.wait_ge(nr["ae"], 2)
            nc.scalar.activation(nb[:, :], na[:, :], ACT.Sqrt).then_inc(nr["s"], 1)
            act.preload_act_table(ACT.Silu)

            def modulate2(t):
                act.wait_ge(fb["hTp"], t + 1)
                wait(act, fb["h2lo"], t)
                for k, c in enumerate((c0, c1)):
                    a = nc.scalar.activation(h2[:, k, :], c[:, :], ACT.Identity,
                                             scale=modt[:, 2, k, bass.ds(t * ST, 1)], bias=modt[:, 3, k, bass.ds(t * ST, 1)])
                a.then_inc(fb["h2"], 1)

            def super_tile(t, last):
                for m in range(MT):
                    act.wait_ge(fb["gate"], t * MT + m + 1)
                    if isinstance(t, int) and t == 0:
                        wait(act, fb["g"], m - 1)
                    else:
                        act.wait_ge(fb["g"], t * MT + m - 1)
                    nc.scalar.activation(sg[:, m % 2, :], big[m % 2][:, 0:512], ACT.Silu).then_inc(fb["sg"], 1)
                    if m == 3 and not last:
                        modulate2(t + 1)

            modulate2(0)
            super_tile(0, False)
            with act.Fori(0, SUPERS // 2 - 1) as u:
                super_tile(u * 2 + 1, False)
                super_tile(u * 2 + 2, False)
            super_tile(SUPERS - 1, True)

        @block.vector
        def _(dve):
            tt, ts, cp = nc.vector.tensor_tensor, nc.vector.tensor_scalar, nc.vector.tensor_copy
            nc.vector.memset(vp[:, :, :, :, :], 0.0).then_inc(pr["vp0"], 1)
            nc.vector.memset(bias_rows[:, :], 0.0).then_inc(pr["rows0"], 1)
            nc.vector.memset(bias_sel[:, :], 0.0).then_inc(pr["sel0"], 1)
            nc.vector.memset(keep[:, :], 1.0).then_inc(pr["keep0"], 1)
            nc.vector.memset(state[:, :, :], 0.0).then_inc(s["state"], 1)
            dve.wait_ge(pr["keep0"], 1)
            nc.vector.memset(vp[:, :, :, 0, D:DV], 1.0).then_inc(pr["vp"], 1)
            for r in range(3):
                a = nc.vector.memset(bias_sel[32 * r:32 * r + 1, :], 1.0)
            a.then_inc(pr["sel"], 1)
            nc.vector.memset(keep[:, 0:TILES:TPB], 0.0).then_inc(pr["keep"], 1)
            nc.vector.memset(fk_hi[:, :, NF:P], 0.0)
            nc.vector.memset(fk_lo[:, :, NF:P], 0.0).then_inc(pr["fkpad"], 1)
            dve.wait_ge(ld_small, 80)
            ts(gu, helmert, gam[:, 0:1], None, ALU.mult).then_inc(pr["gu"], 1)
            ts(bet_bc, ident, 0.0, bet[:, 0:1], ALU.mult, ALU.add).then_inc(pr["betbc"], 1)
            dve.wait_ge(pr["siluc"], 1)
            cp(silu_cb[:, :, :, :], silu_c[:, :, :].unsqueeze(3).broadcast_to([P, KT, BATCH, P])).then_inc(pr["silucb"], 1)
            dve.wait_ge(ld_x, 16 * BATCH)
            with dve.Fori(0, TILES) as t:
                nc.vector.bn_stats(bn[:, bass.ds(t, 1), :].rearrange("p a d -> p (a d)"),
                                   xs[:, bass.ds(t, 1), :].rearrange("p a d -> p (a d)")).then_inc(pr["bn"], 1)
            dve.wait_ge(pr["bn"], TILES)
            dve.wait_ge(pr["wqkhi"], 1)
            for k, c in enumerate((c0, c1)):
                a = tt(wqk_lo[:, k, :], c[:, :], wqk_hi[:, k, :].bitcast(F32), ALU.subtract)
            a.then_inc(pr["wqklo"], 1)
            dve.wait_ge(pr["wvohi"], 1)
            tt(wvo_lo[:, :, :, :], w_in[:, 2:4, :, :], wvo_hi[:, :, :, :].bitcast(F32), ALU.subtract).then_inc(pr["wvolo"], 1)
            dve.wait_ge(pr["bias"], 1)
            b_full = big[0][:, 512:512 + P]
            cp(bias_p[:, 0, :], b_full).then_inc(pr["bp1"], 1)
            dve.wait_ge(pr["bp1"], 1)
            tt(bias_r[:, :], b_full, bias_p[:, 0, :], ALU.subtract).then_inc(pr["br1"], 1)
            dve.wait_ge(pr["br1"], 1)
            cp(bias_p[:, 1, :], bias_r[:, :]).then_inc(pr["bp2"], 1)
            dve.wait_ge(pr["bp2"], 1)
            tt(bias_p[:, 2, :], bias_r[:, :], bias_p[:, 1, :], ALU.subtract).then_inc(pr["bp3"], 1)
            dve.wait_ge(pr["bp3"], 1)
            for r in range(3):
                cp(bias_rows[32 * r:32 * r + 1, :].rearrange("p (g n) -> p g n", g=4),
                   bias_p[32 * r:32 * r + 1, r, :].unsqueeze(1).broadcast_to([1, 4, P])).then_inc(pr["rows"], 1)
            dve.wait_ge(pr["mods"], 1)
            for j in range(4):
                src = big[0][:, j * KT * BATCH:(j + 1) * KT * BATCH].rearrange("p (k b) -> p k b", k=KT)
                for k in range(KT):
                    a = ts(modt[:, j, k, :].rearrange("p (b t) -> p b t", b=BATCH),
                           src[:, k, :].unsqueeze(2).broadcast_to([P, BATCH, TPB]), 1.0 if j % 2 == 0 else 0.0, None, ALU.add)
                a.then_inc(pr["modt"], 1)
            dve.wait_ge(pr["gabs"], 1)
            for j in range(2):
                src = big[1][:, :] if j == 0 else acc[:, :, :].rearrange("p a n -> p (a n)")
                cols = slice(j * BATCH * HID, (j + 1) * BATCH * HID)
                a = ts(gtmp[0][:, cols], src, 0.0, 2.0, ALU.is_ge, ALU.mult)
            a.then_inc(pr["g1"], 1)
            b = ts(gtmp[1], gtmp[1], 0.25, None, ALU.max)
            b.then_inc(pr["g2"], 1)
            dve.wait_ge(pr["g1"], 1)
            dve.wait_ge(pr["g2"], 1)
            nc.vector.scalar_tensor_tensor(gates[:, :, :, :].rearrange("p j b n -> p (j b n)"), gtmp[0], -1.0,
                                           gtmp[1], ALU.add, ALU.mult).then_inc(pr["gfin"], 1)
            dve.wait_ge(pr["gfin"], 1)
            dve.wait_ge(pr["rows"], 3)

            def norms(time):
                m_e, v_e, m_o, v_o = (bn[:, :, i] for i in (1, 2, 4, 5))
                tt(nd[:, :], m_e, m_o, ALU.add).then_inc(nr["m"], 1)
                dve.wait_ge(nr["m"], time)
                ts(mean[:, :], nd[:, :], 0.5, None, ALU.mult).then_inc(nr["mean"], 1)
                tt(na[:, :], v_e, v_o, ALU.add).then_inc(nr["v"], 1)
                dve.wait_ge(nr["mean"], time)
                tt(nd[:, :], m_e, m_o, ALU.subtract).then_inc(nr["d"], 1)
                dve.wait_ge(nr["d"], time)
                nc.vector.scalar_tensor_tensor(rstd[:, :], nd[:, :], 0.25, nd[:, :], ALU.mult, ALU.mult).then_inc(nr["d2"], 1)
                dve.wait_ge(nr["v"], time)
                dve.wait_ge(nr["d2"], time)
                nc.vector.scalar_tensor_tensor(nd[:, :], na[:, :], 1.0 / HID, rstd[:, :], ALU.mult, ALU.add).then_inc(nr["a"], 1)
                dve.wait_ge(nr["a"], time)
                ts(na[:, :], nd[:, :], LN_EPS, None, ALU.add).then_inc(nr["ae"], 1)
                dve.wait_ge(nr["s"], time)
                nc.vector.reciprocal(nd[:, :], nb[:, :]).then_inc(nr["y"], 1)
                dve.wait_ge(nr["y"], time)
                nc.vector.scalar_tensor_tensor(nb[:, :], nd[:, :], -0.5, nd[:, :], ALU.mult, ALU.mult).then_inc(nr["t"], 1)
                dve.wait_ge(nr["t"], time)
                tt(rstd[:, :], nb[:, :], na[:, :], ALU.mult).then_inc(nr["u"], 1)
                dve.wait_ge(nr["u"], time)
                nc.vector.scalar_tensor_tensor(rstd[:, :], rstd[:, :], 1.5, nd[:, :], ALU.add, ALU.mult).then_inc(nr["r"], 1)
                dve.wait_ge(nr["r"], time)

            def row(n):
                return xs[:, bass.ds(n, 1), :].rearrange("p a d -> p (a d)")

            def layer_norm(n):
                wait(dve, s["xT"], n)
                ts(xn[:, :], row(n), mean[:, bass.ds(n, 1)], rstd[:, bass.ds(n, 1)],
                   ALU.subtract, ALU.mult).then_inc(s["xn"], 1)

            def split_h(n):
                dve.wait_ge(s["hT"], n + 1)
                wait(dve, s["v"], n)
                cp(h_hi[:, :, :], hT[:, :, :]).then_inc(s["h_hi"], 1)
                dve.wait_ge(s["h_hi"], n + 1)
                tt(h_lo[:, :, :], hT[:, :, :], h_hi[:, :, :].bitcast(F32), ALU.subtract).then_inc(s["h_split"], 1)

            def head_sums(n):
                dve.wait_ge(s["sq"], n + 1)
                nc.vector.tensor_reduce(rt[:, :], sq[:, :, :], axis=AX.X, op=ALU.add).then_inc(s["ss"], 1)
                dve.wait_ge(s["ss"], n + 1)
                ts(ra[:, :], rt[:, :], 1.0 / D, LN_EPS, ALU.mult, ALU.add).then_inc(s["ra"], 1)

            def head_norms(n, ms_of=None, b=0):
                part = [ms[:, b, i, :, :].rearrange("p h d -> p (h d)") for i in range(PARTS)]
                rest = ms_r[:, :, :].rearrange("p h d -> p (h d)")
                m = ms_of
                if n is not None:
                    dve.wait_ge(s["rs"], n + 1)
                    nc.vector.reciprocal(ry[:, :], rs[:, :]).then_inc(s["ry0"], 1)
                if m is not None:
                    dve.wait_ge(s["msp"], m + 1)
                    wait(dve, s["accp1"], m - 1)
                    ts(part[0], c2[:, 0:HEADS * DV], keep[:, bass.ds(m, 1)], None, ALU.mult).then_inc(s["ms1"], 1)
                if n is not None:
                    dve.wait_ge(s["ry0"], n + 1)
                    nc.vector.scalar_tensor_tensor(rt[:, :], ry[:, :], -0.5, ry[:, :], ALU.mult,
                                                   ALU.mult).then_inc(s["rt0"], 1)
                if m is not None:
                    dve.wait_ge(s["ms1"], m + 1)
                    nc.vector.scalar_tensor_tensor(rest, c2[:, 0:HEADS * DV], keep[:, bass.ds(m, 1)], part[0],
                                                   ALU.mult, ALU.subtract).then_inc(s["msr"], 1)
                if n is not None:
                    dve.wait_ge(s["rt0"], n + 1)
                    tt(rt[:, :], rt[:, :], ra[:, :], ALU.mult).then_inc(s["rt1"], 1)
                if m is not None:
                    dve.wait_ge(s["msr"], m + 1)
                    cp(part[1], rest).then_inc(s["ms2"], 1)
                if n is not None:
                    dve.wait_ge(s["rt1"], n + 1)
                    nc.vector.scalar_tensor_tensor(rt[:, :], rt[:, :], 1.5, ry[:, :], ALU.add, ALU.mult).then_inc(s["ry"], 1)
                if m is not None:
                    dve.wait_ge(s["ms2"], m + 1)
                    tt(part[2], rest, part[1], ALU.subtract).then_inc(s["ms3"], 1)
                if n is not None:
                    dve.wait_ge(s["ry"], n + 1)
                    tt(qn[:, :, :], c0[:, :].rearrange("p (h d) -> p h d", d=D),
                       rt[:, :].unsqueeze(2).broadcast_to([P, 2 * HEADS, D]), ALU.mult).then_inc(s["qn"], 1)
                    dve.wait_ge(s["qn"], n + 1)
                    wait(dve, s["qTp"], n)
                    wait(dve, s["kTp"], n)
                    cp(q16[:, :, 0:2, :], qn[:, 0:HEADS, :].unsqueeze(2).broadcast_to([P, HEADS, 2, D])).then_inc(s["q_hi"], 1)
                    cp(k16[:, :, 0:4:2, :], qn[:, HEADS:, :].unsqueeze(2).broadcast_to([P, HEADS, 2, D])).then_inc(s["k_hi"], 1)

            def split_v(n, b):
                dve.wait_ge(s["v1"], n + 1)
                wait(dve, s["v3"], n)
                tt(v_r1[:, :, :], c2[:, 0:HID].rearrange("p (h d) -> p h d", d=D), vp[:, b, :, 0, 0:D],
                   ALU.subtract).then_inc(s["vr1"], 1)
                dve.wait_ge(s["vr1"], n + 1)
                cp(vp[:, b, :, 1, 0:D], v_r1[:, :, :]).then_inc(s["v2"], 1)

            def update_state(n):
                dve.wait_ge(s["sdp"], n + 1)
                nc.vector.scalar_tensor_tensor(state[:, :, :].rearrange("p h d -> p (h d)"),
                                               state[:, :, :].rearrange("p h d -> p (h d)"), keep[:, bass.ds(n, 1)],
                                               c2[:, 0:HEADS * DV], ALU.mult, ALU.add).then_inc(s["state"], 1)

            def normalize(n):
                dve.wait_ge(s["accp1"], n + 1)
                ts(den[:, :], acc_h[:, :, D], D * ATT_EPS, None, ALU.add).then_inc(s["den"], 1)
                dve.wait_ge(s["den"], n + 1)
                nc.vector.reciprocal(rden[:, :], den[:, :]).then_inc(s["rden"], 1)
                dve.wait_ge(s["rden"], n + 1)
                tt(o_n[:, :, :], acc_h[:, :, 0:D], rden[:, :].unsqueeze(2).broadcast_to([P, HEADS, D]),
                   ALU.mult).then_inc(s["o_n"], 1)

            def o_lo(n):
                dve.wait_ge(s["oT_hi"], n + 1)
                tt(oT_lo[:, :, :].rearrange("p k n -> p (k n)"), acc[:, 0, 0:HID],
                   oT_hi[:, :, :].rearrange("p k n -> p (k n)").bitcast(F32), ALU.subtract).then_inc(s["oT_lo"], 1)

            def gate_y(n):
                dve.wait_ge(s["y"], n + 1)
                wait(dve, s["x1"], n)
                tt(yg[:, :], c1[:, 0:HID], gates[:, 0, bass.ds(n // TPB, 1), :].rearrange("p a d -> p (a d)"),
                   ALU.mult).then_inc(s["yg"], 1)

            def stats2(n):
                dve.wait_ge(s["x1"], n + 1)
                nc.vector.bn_stats(bn[:, bass.ds(n, 1), :].rearrange("p a d -> p (a d)"), row(n)).then_inc(s["bn2"], 1)

            def low(name, n, i, w=P):
                full, hi, lo = {"fk": (fk, fk_hi, fk_lo), "at": (at, at_hi, at_lo), "fq": (fq, fq_hi, fq_lo)}[name]
                hs = slice(i * HALF, (i + 1) * HALF)
                dve.wait_ge(s[f"{name}h{i}"], n + 1)
                tt(lo[:, hs, 0:w], full[:, hs, 0:w], hi[:, hs, 0:w], ALU.subtract).then_inc(s[f"{name}l{i}"], 1)

            def step(n, b, front, back, back2):
                dve.wait_ge(s["qTp"], n + 1)
                cp(qT[:, :, :].rearrange("p j n -> p (j n)"), c0[:, :].bitcast(F16)).then_inc(s["qT"], 1)
                if back:
                    low("at", n - 1, 1)
                if back2:
                    o_lo(n - 2)
                split_v(n, b)
                if front:
                    split_h(n + 1)
                low("fk", n, 0, NF)
                if front:
                    head_sums(n + 1)
                if back2:
                    gate_y(n - 2)
                low("fk", n, 1, NF)
                head_norms(n + 1 if front else None, n, b)
                if back:
                    normalize(n - 1)
                if front:
                    update_state(n)
                low("fq", n, 0)
                low("at", n, 0)
                if front and not (isinstance(n, int) and n == TILES - 2):
                    layer_norm(n + 2)
                if back2:
                    stats2(n - 2)

            dve.wait_ge(pr["vp"], 1)
            dve.wait_ge(pr["fkpad"], 1)
            dve.wait_ge(pr["keep"], 1)
            norms(1)
            layer_norm(0)
            split_h(0)
            head_sums(0)
            head_norms(0)
            layer_norm(1)
            for n in range(4):
                step(n, n % 2, True, n > 0, n > 1)
            with dve.Fori(2, TILES // 2 - 1) as u:
                step(u * 2, 0, True, True, True)
                step(u * 2 + 1, 1, True, True, True)
            step(TILES - 2, 0, True, True, True)
            step(TILES - 1, 1, False, True, True)
            low("at", TILES - 1, 1)
            o_lo(TILES - 2)
            gate_y(TILES - 2)
            normalize(TILES - 1)
            o_lo(TILES - 1)
            stats2(TILES - 2)
            gate_y(TILES - 1)
            stats2(TILES - 1)

            dve.wait_ge(s["bn2"], TILES)
            norms(2)

            def layer_norm2(t):
                wait(dve, fb["hTp"], t)
                for i in range(ST):
                    a = ts(xn2[:, i, :], row(t * ST + i), mean[:, bass.ds(t * ST + i, 1)],
                           rstd[:, bass.ds(t * ST + i, 1)], ALU.subtract, ALU.mult)
                a.then_inc(fb["xn2"], 1)

            def split_h2(t, buf):
                dve.wait_ge(fb["h2"], t + 1)
                cp(h2_hi[buf], h2[:, :, :]).then_inc(fb["h2hi"], 1)
                dve.wait_ge(fb["h2hi"], t + 1)
                tt(h2_lo[buf], h2[:, :, :], h2_hi[buf].bitcast(F32), ALU.subtract).then_inc(fb["h2lo"], 1)

            def finish(t):
                dve.wait_ge(fb["down"], t + 1)
                wait(dve, fb["ob"], t)
                for i in range(ST):
                    a = tt(yb[:, i, :], acc[:, i // 2, (i % 2) * HID:(i % 2 + 1) * HID],
                           gates[:, 1, bass.ds(t // (TPB // ST), 1), :].rearrange("p a d -> p (a d)"), ALU.mult)
                a.then_inc(fb["yb"], 1)

            def super_tile(t, buf, first, last):
                for m in range(MT):
                    i = m % 2
                    dve.wait_ge(fb["sg"], t * MT + m + 1)
                    dve.wait_ge(fb["up"], t * MT + m + 1)
                    tt(g[:, i, :], big[i][:, 512:1024], sg[:, i, :], ALU.mult).then_inc(fb["g"], 1)
                    dve.wait_ge(fb["g"], t * MT + m + 1)
                    cp(g_hi[:, i, :], g[:, i, :]).then_inc(fb["ghi"], 1)
                    dve.wait_ge(fb["ghi"], t * MT + m + 1)
                    tt(g_lo[:, i, :], g[:, i, :], g_hi[:, i, :].bitcast(F32), ALU.subtract).then_inc(fb["glo"], 1)
                    if m == 0 and not last:
                        layer_norm2(t + 1)
                    if m == 1 and not first:
                        finish(t - 1)
                    if m == 4 and not last:
                        split_h2(t + 1, 1 - buf)

            layer_norm2(0)
            split_h2(0, 0)
            super_tile(0, 0, True, False)
            with dve.Fori(0, SUPERS // 2 - 1) as u:
                super_tile(u * 2 + 1, 1, False, False)
                super_tile(u * 2 + 2, 0, False, False)
            super_tile(SUPERS - 1, 1, False, True)
            finish(SUPERS - 1)

        @block.gpsimd
        def _(pool):
            nc.gpsimd.memset(tick[:, :], 0.0).then_inc(pr["tick"], 1)
            pool.wait_ge(pr["tick"], 1)

            def low_parts(n):
                pool.wait_ge(s["q_hi"], n + 1)
                nc.gpsimd.tensor_tensor(q16[:, :, 2:4, :], qn[:, 0:HEADS, :].unsqueeze(2).broadcast_to([P, HEADS, 2, D]),
                                        q16[:, :, 0:2, :], ALU.subtract).then_inc(s["q_lo"], 1)
                pool.wait_ge(s["k_hi"], n + 1)
                nc.gpsimd.tensor_tensor(k16[:, :, 1:4:2, :], qn[:, HEADS:, :].unsqueeze(2).broadcast_to([P, HEADS, 2, D]),
                                        k16[:, :, 0:4:2, :], ALU.subtract).then_inc(s["k_lo"], 1)

            def mask(n):
                for i in range(2):
                    a = at[:, i * HALF:(i + 1) * HALF, :]
                    pool.wait_ge(s[f"at{i}"], n + 1)
                    nc.gpsimd.tensor_tensor(tick[:, 2 + i:3 + i], tick[:, 0:1], tick[:, 1:2], ALU.add).then_inc(pr["tick"], 1)
                    nc.gpsimd.affine_select(out=a, in_=a, pattern=[[0, HALF], [1, P]], compare_op=ALU.is_ge, fill=0.0,
                                            base=0, channel_multiplier=-1).then_inc(s[f"am{i}"], 1)

            def residual(n):
                pool.wait_ge(s["yg"], n + 1)
                x1 = xs[:, bass.ds(n, 1), :].rearrange("p a d -> p (a d)")
                nc.gpsimd.tensor_tensor(x1, x1, yg[:, :], ALU.add).then_inc(s["x1"], 1)

            def third_v(n, b):
                pool.wait_ge(s["v2"], n + 1)
                nc.gpsimd.tensor_tensor(vp[:, b, :, 2, 0:D], v_r1[:, :, :], vp[:, b, :, 1, 0:D], ALU.subtract).then_inc(s["v3"], 1)

            def low_fq1(n):
                pool.wait_ge(s["fqh1"], n + 1)
                hs = slice(HALF, HEADS)
                nc.gpsimd.tensor_tensor(fq_lo[:, hs, :], fq[:, hs, :], fq_hi[:, hs, :], ALU.subtract).then_inc(s["fql1"], 1)

            def step(n, b, front, back, back2):
                third_v(n, b)
                mask(n)
                if back2:
                    residual(n - 2)
                if front:
                    low_parts(n + 1)
                low_fq1(n)

            low_parts(0)
            for n in range(4):
                step(n, n % 2, True, n > 0, n > 1)
                if n < 3:
                    pool.wait_ge(fb["wfh"], n + 1)
                    nc.gpsimd.tensor_tensor(wf_lo[:, n, :], raw, wf_hi[:, n, :].bitcast(F32),
                                            ALU.subtract).then_inc(fb["wfl"], 1)
            with pool.Fori(2, TILES // 2 - 1) as u:
                step(u * 2, 0, True, True, True)
                step(u * 2 + 1, 1, True, True, True)
            step(TILES - 2, 0, True, True, True)
            step(TILES - 1, 1, False, True, True)
            residual(TILES - 2)
            residual(TILES - 1)

            def finish(t):
                pool.wait_ge(fb["yb"], t + 1)
                wait(pool, fb["stored"], t * 16)
                nc.gpsimd.tensor_tensor(ob[:, :, :], xs[:, bass.ds(t * ST, ST), :], yb[:, :, :], ALU.add).then_inc(fb["ob"], 1)

            finish(0)
            with pool.Fori(1, SUPERS) as t:
                finish(t)


def kernel(L0_attn_hidden_states, L0_attn_Wq, L0_attn_Wk, L0_attn_Wv, L0_attn_Wo, L0_attn_gamma, L0_attn_beta,
           L0_ffn_w_gate, L0_ffn_w_up, L0_ffn_w_down, L0_c, L0_wmod):
    import numpy as _np
    import concourse.bacc as _bacc
    from concourse.bass_utils import run_bass_kernel_spmd as _run

    const32, const16 = shape_constants()
    arrays = {
        "in_x": _np.asarray(L0_attn_hidden_states).reshape(BATCH * SEQ, HID),
        "in_wq": _np.asarray(L0_attn_Wq),
        "in_wk": _np.asarray(L0_attn_Wk),
        "in_wv_t": _np.asarray(L0_attn_Wv).T,
        "in_wo_t": _np.asarray(L0_attn_Wo).T,
        "in_gamma": _np.tile(_np.asarray(L0_attn_gamma), P // D).reshape(P, 1),
        "in_beta": _np.tile(_np.asarray(L0_attn_beta), P // D).reshape(P, 1),
        "in_wg_t": _np.asarray(L0_ffn_w_gate).T,
        "in_wu_t": _np.asarray(L0_ffn_w_up).T,
        "in_wd_t": _np.asarray(L0_ffn_w_down).T,
        "in_c_t": _np.asarray(L0_c).T,
        "in_wmod": _np.asarray(L0_wmod),
        "const32": const32,
        "const16": const16,
    }
    arrays = {k: _np.ascontiguousarray(a) for k, a in arrays.items()}
    nc = _bacc.Bacc("TRN2", target_bir_lowering=False, num_devices=1)
    args = [nc.dram_tensor(k, a.shape, mybir.dt.from_np(a.dtype), kind="ExternalInput").ap() for k, a in arrays.items()]
    out = nc.dram_tensor("out", (BATCH * SEQ, HID), mybir.dt.float32, kind="ExternalOutput").ap()
    build(nc, *args, out)
    r = _run(nc, [arrays], core_ids=[0])
    return r.results[0]["out"].reshape(BATCH, SEQ, HID)
```

```python
import numpy as np

import concourse.bass as bass
from concourse import mybir
from concourse.alu_op_type import AluOpType as ALU

P = 128
BATCH, SEQ, HID = 4, 1024, 256
HEADS, D = 16, 16
FFN = 1024
LN_EPS = 1e-5
ATT_EPS = 1e-5
KT = HID // P
TILES = BATCH * SEQ // P
TPB = SEQ // P
R = D - 1
NF = R * (R + 1) // 2
PARTS = 3
DV = D + 1
PAIRS = HEADS // 2
HALF = HEADS // 2
MT = FFN // P
ST = 4
SUPERS = TILES // ST


def shape_constants():
    helmert = np.zeros((D, D))
    for i in range(R):
        helmert[: i + 1, i] = 1.0
        helmert[i + 1, i] = -(i + 1.0)
        helmert[:, i] /= np.sqrt((i + 1.0) * (i + 2.0))
    block = np.kron(np.eye(P // D), helmert)
    feat = np.zeros((D, P))
    mono = np.zeros((NF, NF))
    m = R
    for i in range(R):
        feat[i, i] = 1.0
        mono[i, i] = 1.0
        for j in range(i + 1, R):
            feat[i, m] = feat[j, m] = 1.0
            mono[m, m], mono[m, i], mono[m, j] = 0.5, -0.5, -0.5
            m += 1
    weight = np.diag([1.0] * R + [2.0] * (NF - R))
    mix = np.zeros((P, P))
    mix[:NF, :NF] = mono.T @ weight @ mono
    zero = np.zeros((D, P))
    uq = np.concatenate([feat, zero, feat, zero] * 2)
    uk = np.zeros((P, 2 * P))
    for e in range(2):
        uk[64 * e:64 * e + D, P * e:P * e + P] = feat
        uk[64 * e + D:64 * e + 2 * D, P * e:P * e + P] = feat
    const32 = np.concatenate([np.eye(P), block, mix], 1).astype(np.float32)
    const16 = np.concatenate([np.eye(P), uq, uk], 1).astype(np.float16)
    return const32, const16


def wait(eng, sem, count):
    if isinstance(count, int) and count <= 0:
        return
    eng.wait_ge(sem, count)


def build(nc, x, w_q, w_k, w_v_t, w_o_t, gamma, beta, w_gate_t, w_up_t, w_down_t, c_t, w_mod, const32, const16, out):
    from contextlib import ExitStack

    F32, F32R = mybir.dt.float32, mybir.dt.float32r
    F16, BF16 = mybir.dt.float16, mybir.dt.bfloat16
    ACT = mybir.ActivationFunctionType
    AX = mybir.AxisListType

    ctx = ExitStack()
    with ctx:
        def sb(name, shape, dt=F32):
            return ctx.enter_context(nc.sbuf_tensor(name, [P] + shape, dt))

        def ps(name, shape, dt=F32):
            return ctx.enter_context(nc.psum_tensor(name, [P] + shape, dt))

        def sem(name):
            return ctx.enter_context(nc.semaphore(name))

        c32 = sb("c32", [3 * P])
        ident, helmert, mix = c32[:, 0:P], c32[:, P:2 * P], c32[:, 2 * P:3 * P]
        c16 = sb("c16", [4 * P], F16)
        ident16, uq, uk = c16[:, 0:P], c16[:, P:2 * P], c16[:, 2 * P:4 * P]
        xs = sb("xs", [TILES, HID])
        wmod = sb("wmod", [KT, 6 * HID])
        raw = wmod[:, :, :].rearrange("p k n -> p (k n)")[:, 0:2 * ST * HID]
        gam, bet = sb("gam", [1]), sb("bet", [1])
        silu_c = sb("silu_c", [KT, BATCH])
        modt = sb("modt", [4, KT, TILES])
        gates = sb("gates", [2, BATCH, HID])
        keep = sb("keep", [TILES])
        bias_rows = sb("bias_rows", [2 * HID], BF16)
        bias_sel = sb("bias_sel", [P], BF16)
        wqk_hi, wqk_lo = sb("wqk_hi", [KT, 2 * HID], F32R), sb("wqk_lo", [KT, 2 * HID], F32R)
        wvo_hi, wvo_lo = sb("wvo_hi", [2, KT, HID], F32R), sb("wvo_lo", [2, KT, HID], F32R)
        wf_hi, wf_lo = sb("wf_hi", [3, 2048], F32R), sb("wf_lo", [3, 2048], F32R)

        tick = sb("tick", [4])
        bn, mean, rstd = sb("bn", [TILES, 6]), sb("mean", [TILES]), sb("rstd", [TILES])
        na, nb, nd = sb("na", [TILES]), sb("nb", [TILES]), sb("nd", [TILES])
        xn = sb("xn", [HID])
        hT = sb("hT", [KT, P])
        h_hi, h_lo = sb("h_hi", [2, KT, P], F32R), sb("h_lo", [2, KT, P], F32R)
        sq = sb("sq", [2 * HEADS, D])
        ra, rs, ry, rt = sb("ra", [2 * HEADS]), sb("rs", [2 * HEADS]), sb("ry", [2 * HEADS]), sb("rt", [2 * HEADS])
        qn = sq
        q16, k16 = sb("q16", [HEADS, 4, D], F16), sb("k16", [HEADS, 4, D], F16)
        vp = sb("vp", [2, HEADS, PARTS, DV], BF16)
        qT, kT = sb("qT", [PAIRS, P], F16), sb("kT", [PAIRS, P], F16)
        fk, fk_hi, fk_lo = sb("fk", [HEADS, P]), sb("fk_hi", [HEADS, P], F16), sb("fk_lo", [HEADS, P], F16)
        at, at_hi, at_lo = sb("at", [HEADS, P]), sb("at_hi", [HEADS, P], F16), sb("at_lo", [HEADS, P], F16)
        fq, fq_hi, fq_lo = sb("fq", [HEADS, P]), sb("fq_hi", [HEADS, P], F16), sb("fq_lo", [HEADS, P], F16)
        state = sb("state", [HEADS, DV])
        ms_r = sb("ms_r", [HEADS, DV])
        v_r1 = ms_r[:, :, 0:D]
        ms = sb("ms", [2, PARTS, HEADS, DV], BF16)
        den, rden, o_n = sb("den", [HEADS]), sb("rden", [HEADS]), sb("o_n", [HEADS, D])
        oT_hi, oT_lo = sb("oT_hi", [KT, P], F32R), sb("oT_lo", [KT, P], F32R)
        yg = sb("yg", [HID])
        h2_hi1, h2_lo1 = sb("h2_hi1", [KT, ST * P], F32R), sb("h2_lo1", [KT, ST * P], F32R)
        h2_hi = [wvo_hi[:, :, :, :].rearrange("p i k n -> p i (k n)"), h2_hi1[:, :, :]]
        h2_lo = [wvo_lo[:, :, :, :].rearrange("p i k n -> p i (k n)"), h2_lo1[:, :, :]]
        g_hi, g_lo = wqk_hi, wqk_lo
        w_in = fq[:, :, :].rearrange("p (i k a) n -> p i k (a n)", i=4, k=KT)
        gu, bet_bc = at[:, 0, :], at[:, 1, :]
        bias_r, bias_p = at[:, 2, :], at_hi[:, 0:3, :].bitcast(BF16)
        silu_cb = at[:, HALF:HEADS, :].rearrange("p (k b) n -> p k b n", k=KT)
        raw_ffn = [[fk[:, :, :].rearrange("p h n -> p (h n)")], [fq[:, :, :].rearrange("p h n -> p (h n)")],
                   [x[:, :, :].rearrange("p h n -> p (h n)").bitcast(F32) for x in (at_hi, at_lo)]]
        sign = raw
        xn2 = raw[:, 0:ST * HID].rearrange("p (i n) -> p i n", i=ST)
        h2 = raw[:, ST * HID:2 * ST * HID].rearrange("p (k n) -> p k n", k=KT)
        sg = fq[:, 0:HALF, :].rearrange("p (k i) n -> p k (i n)", k=2)
        g = fq[:, HALF:HEADS, :].rearrange("p (k i) n -> p k (i n)", k=2)
        yb = fk[:, 0:HALF, :].rearrange("p (i k) n -> p i (k n)", i=ST)
        ob = fk[:, HALF:HEADS, :].rearrange("p (i k) n -> p i (k n)", i=ST)

        big = [ps("big0", [1024]), ps("big1", [1024])]
        acc = ps("acc", [2, 512])
        c0, c1 = ps("c0", [512]), ps("c1", [512])
        c2 = acc[:, 1, :]
        acc_h = acc[:, 0, 0:HEADS * DV].rearrange("p (h d) -> p h d", h=HEADS)
        c2_h = acc[:, 1, 0:HEADS * DV].rearrange("p (h d) -> p h d", h=HEADS)

        ld_small, ld_mod1, ld_mod2, ld_qk, ld_vo = (
            sem(n) for n in ("ld_small", "ld_mod1", "ld_mod2", "ld_qk", "ld_vo"))
        ld_ffn = [sem(f"ld_ffn{i}") for i in range(3)]
        ld_x = [sem(f"ld_x{b}") for b in range(BATCH)]
        pr = {n: sem("pr_" + n) for n in (
            "gu", "betbc", "siluc", "silucb", "mods", "gates", "wqk", "bias", "modt", "g1", "g2", "gfin", "wqkhi",
            "bp1", "br1", "bp2", "bp3", "rows0", "rows", "sel0", "sel", "vp0", "vp", "wvohi", "wvolo", "wqklo", "keep0", "keep",
            "fkpad", "gabs", "tick", "bn", "root")}
        nr = {n: sem("nr_" + n) for n in ("m", "mean", "d", "d2", "v", "a", "ae", "s", "y", "t", "u", "r")}
        names = ("xn", "xT", "hT", "h_hi", "h_split", "qk", "v", "sq",
                 "ss", "ra", "rs", "ry0", "rt0", "rt1", "ry", "qn", "q_hi", "k_hi", "q_lo", "k_lo", "v1", "vr1", "v2", "v3",
                 "qTp", "kTp", "qT", "kT", "fk0p", "fk1p", "fk0", "fk1", "fkh0", "fkh1", "fkl0", "fkl1",
                 "sc0p", "sc1p", "at0", "at1", "am0", "am1", "ath0", "ath1", "atl0", "atl1",
                 "fq0p", "fq1p", "fq0", "fq1", "fqh0", "fqh1", "fql0", "fql1", "intra0", "intra1", "accp0", "accp1", "sdp0", "sdp1", "state",
                 "msp", "ms1", "msr", "ms2", "ms3",
                 "den", "rden", "o_n", "oTp", "oT_hi", "oT_lo", "y", "yg", "x1", "bn2")
        s = {n: sem("s_" + n) for n in names}
        fb = {n: sem("f_" + n) for n in (
            "wfh", "wfl", "xn2", "hTp", "h2", "h2hi", "h2lo",
            "gate", "up", "sg", "g", "ghi", "glo", "down0", "down", "yb", "ob", "stored", "yb_last", "ob_last")}

        block = ctx.enter_context(nc.Block())

        @block.sync
        def _(sp):
            sp.dma_start(silu_c[:, :, :], c_t.rearrange("(k p) b -> p k b", p=P)).then_inc(ld_small, 16)
            sp.dma_start(c32[:, :], const32).then_inc(ld_small, 16)
            sp.dma_start(c16[:, :], const16).then_inc(ld_small, 16)
            sp.dma_start(gam[:, :], gamma).then_inc(ld_small, 16)
            sp.dma_start(bet[:, :], beta).then_inc(ld_small, 16)
            mod = w_mod.rearrange("(k p) n -> p k n", p=P)
            sp.dma_start(wmod[:, :, 0:2 * HID], mod[:, :, 0:2 * HID]).then_inc(ld_mod1, 16)
            for b in range(BATCH):
                sp.dma_start(xs[:, TPB * b:TPB * (b + 1), :],
                             x[SEQ * b:SEQ * (b + 1), :].rearrange("(t p) d -> p t d", p=P)).then_inc(ld_x[b], 16)
                if b == 0:
                    for i, w in enumerate((w_q, w_k, w_v_t, w_o_t)):
                        sp.dma_start(w_in[:, i, :, :], w.rearrange("(k p) n -> p k n", p=P)).then_inc(
                            ld_qk if i < 2 else ld_vo, 16)
                    sp.dma_start(wmod[:, :, 2 * HID:], mod[:, :, 2 * HID:]).then_inc(ld_mod2, 16)
            sp.dma_start(raw_ffn[0][0].rearrange("p (k n) -> p k n", k=KT),
                         w_gate_t.rearrange("(k p) n -> p k n", p=P)).then_inc(ld_ffn[0], 16)
            sp.wait_ge(pr["wvolo"], 1)
            sp.dma_start(raw_ffn[1][0].rearrange("p (k n) -> p k n", k=KT),
                         w_up_t.rearrange("(k p) n -> p k n", p=P)).then_inc(ld_ffn[1], 16)
            sp.wait_ge(pr["rows"], 3)
            for i, half in enumerate(raw_ffn[2]):
                sp.dma_start(half.rearrange("p (k n) -> p k n", k=MT // 2),
                             w_down_t[i * FFN // 2:(i + 1) * FFN // 2, :].rearrange("(k p) n -> p k n", p=P)).then_inc(
                                 ld_ffn[2], 16)
            with sp.Fori(0, SUPERS - 1) as t:
                sp.wait_ge(fb["ob"], t + 1)
                sp.dma_start(out[bass.ds(t * ST * P, ST * P), :].rearrange("(t p) d -> p t d", p=P),
                             ob[:, :, :]).then_inc(fb["stored"], 16)
            for i in (0, 2):
                t = (SUPERS - 1) * ST + i
                sp.wait_ge(fb["ob_last"], 1 + i // 2)
                sp.dma_start(out[t * P:(t + 2) * P, :].rearrange("(t p) d -> p t d", p=P),
                             ob[:, i:i + 2, :]).then_inc(fb["stored"], 16)
            sp.wait_ge(fb["stored"], 16 * (SUPERS + 1))

        def split_product(out_ap, a_hi, a_lo, b_hi, b_lo, ktiles, first=True, last=True):
            mm = None
            for k in range(ktiles):
                for i, (a, b) in enumerate(((a_hi, b_hi), (a_lo, b_hi), (a_hi, b_lo))):
                    mm = nc.tensor.matmul(out_ap, a(k), b(k), start=first and k == 0 and i == 0,
                                          stop=last and k == ktiles - 1 and i == 2, skip_group_check=True)
            return mm

        @block.tensor
        def _(pe):
            def modulations(params):
                for j, param in params:
                    for k in range(KT):
                        for i in range(KT):
                            o = (j * KT + k) * BATCH
                            mm = nc.tensor.matmul(big[0][:, o:o + BATCH],
                                                  wmod[:, i, param * HID + k * P:param * HID + (k + 1) * P],
                                                  silu_c[:, i, :], start=i == 0, stop=i == KT - 1)
                mm.then_inc(pr["mods"], 1)

            pe.wait_ge(pr["betbc"], 1)
            nc.tensor.matmul(acc[:, 0, 0:P], bet_bc, helmert, start=True, stop=True).then_inc(pr["bias"], 1)
            pe.wait_ge(pr["siluc"], 1)
            pe.wait_ge(ld_mod1, 16)
            modulations(((0, 1), (1, 0)))
            pe.wait_ge(ld_qk, 32)
            pe.wait_ge(pr["gu"], 1)
            for qk in range(2):
                for ko in range(KT):
                    for k in range(KT):
                        mm = nc.tensor.matmul(big[1][:, k * 2 * HID + qk * HID + ko * P:k * 2 * HID + qk * HID + (ko + 1) * P],
                                              w_in[:, qk, ko, k * P:(k + 1) * P], gu, start=True, stop=True)
            mm.then_inc(pr["wqk"], 1)

            def gate_rows():
                pe.wait_ge(pr["silucb"], 1)
                pe.wait_ge(pr["wqklo"], 1)
                pe.wait_ge(pr["br1"], 1)
                for j, param in enumerate((2, 5)):
                    for b in range(BATCH):
                        dst = (big[1][:, b * HID:(b + 1) * HID] if j == 0 else
                               acc[:, b // 2, (b % 2) * HID:(b % 2 + 1) * HID])
                        for i in range(KT):
                            mm = nc.tensor.matmul(dst, silu_cb[:, i, b, :], wmod[:, i, param * HID:(param + 1) * HID],
                                                  start=i == 0, stop=i == KT - 1)
                    mm.then_inc(pr["gates"], 1)

            def x_transpose(n):
                pe.wait_ge(s["xn"], n + 1)
                for k in range(KT):
                    mm = nc.tensor.transpose(c0[:, k * P:(k + 1) * P], xn[:, k * P:(k + 1) * P], ident)
                mm.then_inc(s["xT"], 1)

            def project_qk(n, b):
                pe.wait_ge(s["h_hi"], n + 1)
                pe.wait_ge(s["h_split"], n + 1)
                nc.tensor.matmul(c0[:, :], bias_sel[:, :], bias_rows[:, :], start=True, stop=False, skip_group_check=True)
                split_product(c0[:, :], lambda k: h_hi[:, b, k, :], lambda k: h_lo[:, b, k, :],
                              lambda k: wqk_hi[:, k, :], lambda k: wqk_lo[:, k, :], KT, first=False).then_inc(s["qk"], 1)

            def project_v(n, b):
                wait(pe, s["oT_lo"], n - 1)
                split_product(c2[:, 0:HID], lambda k: h_hi[:, b, k, :], lambda k: h_lo[:, b, k, :],
                              lambda k: wvo_hi[:, 0, k, :], lambda k: wvo_lo[:, 0, k, :], KT).then_inc(s["v"], 1)

            def by_parts(out_ap, hi, lo, parts, start, stop):
                for i, (a, p) in enumerate(((hi, 0), (hi, 1), (hi, 2), (lo, 0), (lo, 1))):
                    mm = nc.tensor.matmul(out_ap, a, parts(p), start=start and i == 0, stop=stop and i == 4,
                                          skip_group_check=True)
                return mm

            def o_transpose(n):
                pe.wait_ge(s["o_n"], n + 1)
                for k in range(KT):
                    mm = nc.tensor.transpose(c2[:, k * P:(k + 1) * P],
                                             o_n[:, :, :].rearrange("p h d -> p (h d)")[:, k * P:(k + 1) * P], ident)
                mm.then_inc(s["oTp"], 1)

            def o_project(n):
                pe.wait_ge(s["oT_hi"], n + 1)
                pe.wait_ge(s["oT_lo"], n + 1)
                split_product(c1[:, 0:HID], lambda k: oT_hi[:, k, :], lambda k: oT_lo[:, k, :],
                              lambda k: wvo_hi[:, 1, k, :], lambda k: wvo_lo[:, 1, k, :], KT).then_inc(s["y"], 1)

            def slot(h):
                return (h % 2) * (HALF // 2) + h // 2

            def inside(n, b, i):
                pe.wait_ge(s["v3"], n + 1)
                pe.wait_ge(s[f"ath{i}"], n + 1)
                pe.wait_ge(s[f"atl{i}"], n + 1)
                for h in range(HALF):
                    a, c = i * HALF + slot(h), i * HALF + h
                    mm = by_parts(acc_h[:, c, :], at_hi[:, a, :], at_lo[:, a, :], lambda p: vp[:, b, c, p, :], False, True)
                mm.then_inc(s[f"intra{i}"], 1)

            def before(n, b, i):
                wait(pe, s["o_n"], n)
                pe.wait_ge(s["ms3"], n + 1)
                pe.wait_ge(s[f"fqh{i}"], n + 1)
                pe.wait_ge(s[f"fql{i}"], n + 1)
                for h in range(HALF):
                    a, c = i * HALF + slot(h), i * HALF + h
                    mm = by_parts(acc_h[:, c, :], fq_hi[:, a, :], fq_lo[:, a, :], lambda p: ms[:, b, p, c, :],
                                  c == 0, False)
                mm.then_inc(s[f"accp{i}"], 1)

            def state_part(n, b, i):
                pe.wait_ge(s["v3"], n + 1)
                pe.wait_ge(s["msr"], n + 1)
                pe.wait_ge(s[f"fkh{i}"], n + 1)
                pe.wait_ge(s[f"fkl{i}"], n + 1)
                for h in range(i * HALF, (i + 1) * HALF):
                    mm = by_parts(c2_h[:, h, :], fk_hi[:, h, :], fk_lo[:, h, :], lambda p: vp[:, b, h, p, :], True, True)
                mm.then_inc(s[f"sdp{i}"], 1)

            def key_features(n, i):
                wait(pe, s[f"fqh{i}"], n)
                for j in range(PAIRS // 2):
                    mm = nc.tensor.matmul(big[i][:, j * 2 * P:(j + 1) * 2 * P], kT[:, i * PAIRS // 2 + j, :], uk,
                                          start=True, stop=True)
                mm.then_inc(s[f"fk{i}p"], 1)

            def scores(n, i, front):
                if front:
                    pe.wait_ge(s[f"fkh{i}"], n + 1)
                else:
                    pe.wait_ge(s[f"fqh{i}"], n)
                for h in range(HALF):
                    j, e = i * PAIRS // 2 + h // 2, 64 * (h % 2)
                    mm = nc.tensor.matmul(big[i][:, slot(h) * P:(slot(h) + 1) * P], kT[e:e + 64, j, :],
                                          qT[e:e + 64, j, :], start=True, stop=True)
                mm.then_inc(s[f"sc{i}p"], 1)

            def query_features(n, i):
                pe.wait_ge(s[f"at{i}"], n + 1)
                for e in range(2):
                    mm = nc.tensor.matmul(big[i][:, e * 512:(e + 1) * 512], uq[64 * e:64 * e + 64, :],
                                          qT[64 * e:64 * e + 64, i * PAIRS // 2:(i + 1) * PAIRS // 2, :],
                                          start=True, stop=True)
                mm.then_inc(s[f"fq{i}p"], 1)

            def step(n, b, front, back, back2):
                wait(pe, s["yg"], n - 2)
                for c, x16, part, done in ((c0, q16, "q_lo", "qTp"), (c1, k16, "k_lo", "kTp")):
                    pe.wait_ge(s[part], n + 1)
                    for j in range(PAIRS):
                        mm = nc.tensor.transpose(c[:, :].bitcast(F16)[:, j * P:(j + 1) * P],
                                                 x16[:, :, :, :].rearrange("p h r d -> p (h r d)")[:, j * P:(j + 1) * P],
                                                 ident16)
                    mm.then_inc(s[done], 1)
                if back:
                    state_part(n - 1, 1 - b, 1)
                if front:
                    pe.wait_ge(s["qT"], n + 1)
                    x_transpose(n + 1)
                if isinstance(n, int) and n == 0:
                    pe.wait_ge(pr["g1"], 1)
                    pe.wait_ge(pr["modt"], 4)
                pe.wait_ge(s["kT"], n + 1)
                if front:
                    key_features(n, 0)
                    key_features(n, 1)
                pe.wait_ge(s["state"], n + 1)
                if back2:
                    o_transpose(n - 2)
                if front:
                    project_qk(n + 1, 1 - b)
                project_v(n, b)
                pe.wait_ge(s["qT"], n + 1)
                scores(n, 0, front)
                if back:
                    before(n - 1, 1 - b, 0)
                scores(n, 1, front)
                query_features(n, 0)
                pe.wait_ge(s["vr1"], n + 1)
                nc.tensor.matmul(c2[:, 0:HEADS * DV], mix, state[:, :, :].rearrange("p h d -> p (h d)"),
                                 start=True, stop=True).then_inc(s["msp"], 1)
                if not front:
                    h2_transpose(0, 0, c0)
                if back:
                    before(n - 1, 1 - b, 1)
                query_features(n, 1)
                if not front:
                    pe.wait_ge(fb["h2"], 1)
                    h2_transpose(0, 1, c0)
                if back:
                    inside(n - 1, 1 - b, 0)
                if back2:
                    o_project(n - 2)
                if back:
                    inside(n - 1, 1 - b, 1)
                if front:
                    state_part(n, b, 0)

            wg = [w[:, 0, :].rearrange("p (k n) -> p k n", k=KT) for w in (wf_hi, wf_lo)]
            wu = [w[:, 1, :].rearrange("p (k n) -> p k n", k=KT) for w in (wf_hi, wf_lo)]
            wd = [w[:, 2, :].rearrange("p (m n) -> p m n", m=MT) for w in (wf_hi, wf_lo)]

            def h2_transpose(t, k, c):
                pe.wait_ge(fb["xn2"], t + 1)
                for i in range(ST):
                    mm = nc.tensor.transpose(c[:, i * P:(i + 1) * P], xn2[:, i, k * P:(k + 1) * P], ident)
                mm.then_inc(fb["hTp"], 1)

            def gate_up(t, m, buf):
                b = big[m % 2]
                if isinstance(t, int) and t == 0:
                    wait(pe, fb["g"], m - 1)
                else:
                    pe.wait_ge(fb["g"], t * MT + m - 1)
                cols = slice(m * P, (m + 1) * P)
                for w, o, done in ((wg, 0, "gate"), (wu, 512, "up")):
                    split_product(b[:, o:o + 512], lambda k: w[0][:, k, cols], lambda k: w[1][:, k, cols],
                                  lambda k: h2_hi[buf][:, k, :], lambda k: h2_lo[buf][:, k, :], KT).then_inc(fb[done], 1)

            def down(t, m):
                pe.wait_ge(fb["ghi"], t * MT + m + 1)
                pe.wait_ge(fb["glo"], t * MT + m + 1)
                if m == 0:
                    wait(pe, fb["yb"], t)
                for i in range(ST):
                    tok = slice(i * P, (i + 1) * P)
                    mm = split_product(acc[:, i // 2, (i % 2) * HID:(i % 2 + 1) * HID],
                                       lambda k: g_hi[:, m % 2, tok], lambda k: g_lo[:, m % 2, tok],
                                       lambda k: wd[0][:, m, :], lambda k: wd[1][:, m, :], 1,
                                       first=m == 0 and i % 2 == 0, last=m == MT - 1)
                if m == MT - 1:
                    mm.then_inc(fb["down"], 1)
                return mm

            def super_tile(t, buf, last):
                pe.wait_ge(fb["h2hi"], t + 1)
                pe.wait_ge(fb["h2lo"], t + 1)
                for m in range(MT):
                    gate_up(t, m, buf)
                    if m > 0:
                        down(t, m - 1)
                    else:
                        down(t - 1, MT - 1)
                    if m == 3 and not last:
                        h2_transpose(t + 1, 0, c0)
                        h2_transpose(t + 1, 1, c1)

            x_transpose(0)
            pe.wait_ge(pr["wqkhi"], 1)
            pe.wait_ge(pr["wqklo"], 1)
            pe.wait_ge(pr["rows"], 3)
            pe.wait_ge(pr["sel"], 1)
            project_qk(0, 0)
            pe.wait_ge(pr["modt"], 2)
            pe.wait_ge(ld_mod2, 16)
            modulations(((2, 4), (3, 3)))
            gate_rows()
            pe.wait_ge(pr["wvohi"], 1)
            pe.wait_ge(pr["wvolo"], 1)
            for n in range(4):
                step(n, n % 2, True, n > 0, n > 1)
            with pe.Fori(2, TILES // 2 - 1) as u:
                step(u * 2, 0, True, True, True)
                step(u * 2 + 1, 1, True, True, True)
            step(TILES - 2, 0, True, True, True)
            step(TILES - 1, 1, False, True, True)
            pe.wait_ge(fb["wfh"], 3)
            pe.wait_ge(fb["wfl"], 3)
            pe.wait_ge(fb["h2hi"], 1)
            pe.wait_ge(fb["h2lo"], 1)
            pe.wait_ge(s["fqh0"], TILES)
            gate_up(0, 0, 1)
            o_transpose(TILES - 2)
            pe.wait_ge(s["fqh1"], TILES)
            gate_up(0, 1, 1)
            pe.wait_ge(s["yg"], TILES - 2)
            o_project(TILES - 2)
            for i in range(2):
                before(TILES - 1, 1, i)
            for i in range(2):
                inside(TILES - 1, 1, i)
            gate_up(0, 2, 1)
            o_transpose(TILES - 1)
            pe.wait_ge(s["yg"], TILES - 1)
            o_project(TILES - 1)
            down(0, 0).then_inc(fb["down0"], 1)
            down(0, 1)
            for m in range(3, MT):
                gate_up(0, m, 1)
                down(0, m - 1)
                if m == 3:
                    pe.wait_ge(s["yg"], TILES)
                    h2_transpose(1, 0, c0)
                    h2_transpose(1, 1, c1)
            with pe.Fori(0, SUPERS // 2 - 1) as u:
                super_tile(u * 2 + 1, 0, False)
                super_tile(u * 2 + 2, 1, False)
            super_tile(SUPERS - 1, 0, True)
            down(SUPERS - 1, MT - 1)

        @block.scalar
        def _(act):
            act.wait_ge(ld_small, 80)
            nc.scalar.activation(silu_c[:, :, :], silu_c[:, :, :], ACT.Silu).then_inc(pr["siluc"], 1)
            act.preload_act_table(ACT.Sqrt)
            def roots(time, first, last):
                act.wait_ge(nr["ae"], time)
                nc.scalar.activation(nb[:, first:last], na[:, first:last], ACT.Sqrt).then_inc(nr["s"], 1)

            def modulate(n):
                act.wait_ge(s["xT"], n + 1)
                wait(act, s["h_split"], n)
                for k in range(KT):
                    a = nc.scalar.activation(hT[:, k, :], c0[:, k * P:(k + 1) * P], ACT.Identity,
                                             scale=modt[:, 0, k, bass.ds(n, 1)], bias=modt[:, 1, k, bass.ds(n, 1)])
                a.then_inc(s["hT"], 1)

            def head_squares(n):
                act.wait_ge(s["qk"], n + 1)
                wait(act, s["q_lo"], n)
                wait(act, s["k_lo"], n)
                nc.scalar.activation(sq[:, :, :].rearrange("p h d -> p (h d)"), c0[:, :], ACT.Square).then_inc(s["sq"], 1)

            def head_roots(n):
                act.wait_ge(s["ra"], n + 1)
                wait(act, s["ry0"], n)
                nc.scalar.activation(rs[:, :], ra[:, :], ACT.Sqrt).then_inc(s["rs"], 1)

            def o_hi(n):
                act.wait_ge(s["oTp"], n + 1)
                wait(act, s["y"], n)
                nc.scalar.activation(oT_hi[:, :, :].rearrange("p k n -> p (k n)"), c2[:, 0:HID],
                                     ACT.Copy).then_inc(s["oT_hi"], 1)

            def flat(t, i, w=P):
                return t[:, i * HALF:(i + 1) * HALF, 0:w]

            def key_features(n, i):
                src = big[i][:, :].rearrange("p (h n) -> p h n", h=HALF)[:, :, 0:NF]
                act.wait_ge(s[f"fk{i}p"], n + 1)
                wait(act, s[f"fkl{i}"], n)
                if isinstance(n, int) and n == 0:
                    act.wait_ge(fb["wfl"], 1)
                nc.scalar.activation(flat(fk, i, NF), src, ACT.Square).then_inc(s[f"fk{i}"], 1)
                wait(act, s[f"sdp{i}"], n)
                nc.scalar.activation(flat(fk_hi, i, NF), src, ACT.Square).then_inc(s[f"fkh{i}"], 1)

            def query_features(n, i):
                src = big[i][:, :].rearrange("p (h n) -> p h n", h=HALF)
                act.wait_ge(s[f"fq{i}p"], n + 1)
                wait(act, s[f"fql{i}"], n)
                if isinstance(n, int) and n == 0:
                    act.wait_ge(fb["wfl"], 2)
                nc.scalar.activation(flat(fq, i), src, ACT.Square).then_inc(s[f"fq{i}"], 1)
                wait(act, s[f"accp{i}"], n)
                nc.scalar.activation(flat(fq_hi, i), src, ACT.Square).then_inc(s[f"fqh{i}"], 1)

            def weights(n, i):
                act.wait_ge(s[f"sc{i}p"], n + 1)
                wait(act, s[f"atl{i}"], n)
                nc.scalar.activation(flat(at, i), big[i][:, :].rearrange("p (h n) -> p h n", h=HALF),
                                     ACT.Square).then_inc(s[f"at{i}"], 1)

            def weights_hi(n, i):
                act.wait_ge(s[f"am{i}"], n + 1)
                wait(act, s[f"intra{i}"], n)
                if isinstance(n, int) and n == 0:
                    act.wait_ge(fb["wfl"], 3)
                nc.scalar.activation(flat(at_hi, i), flat(at, i), ACT.Copy).then_inc(s[f"ath{i}"], 1)

            def modulate2(t, k, c):
                wait(act, fb["h2lo"], t)
                act.wait_ge(fb["hTp"], t * 2 + k + 1)
                nc.scalar.activation(h2[:, k, :], c[:, :], ACT.Identity, scale=modt[:, 2, k, bass.ds(t * ST, 1)],
                                     bias=modt[:, 3, k, bass.ds(t * ST, 1)]).then_inc(fb["h2"], 1)

            def silu(t, m):
                act.wait_ge(fb["gate"], t * MT + m + 1)
                if isinstance(t, int) and t == 0:
                    wait(act, fb["g"], m - 1)
                else:
                    act.wait_ge(fb["g"], t * MT + m - 1)
                nc.scalar.activation(sg[:, m % 2, :], big[m % 2][:, 0:512], ACT.Silu).then_inc(fb["sg"], 1)

            def super_tile(t, last):
                for m in range(MT):
                    silu(t, m)
                    if m == 3 and not last:
                        modulate2(t + 1, 0, c0)
                        modulate2(t + 1, 1, c1)

            def step(n, b, front, back, back2):
                act.wait_ge(s["kTp"], n + 1)
                nc.scalar.activation(kT[:, :, :].rearrange("p j n -> p (j n)"), c1[:, :].bitcast(F16),
                                     ACT.Copy).then_inc(s["kT"], 1)
                if front:
                    modulate(n + 1)
                if front:
                    key_features(n, 0)
                if back2:
                    o_hi(n - 2)
                if front:
                    key_features(n, 1)
                if front:
                    head_squares(n + 1)
                else:
                    roots(3, 0, TILES - ST)
                act.wait_ge(s["v"], n + 1)
                wait(act, s["intra1"], n - 1)
                wait(act, s["sdp1"], n - 1)
                nc.scalar.activation(vp[:, b, :, 0, 0:D], c2[:, 0:HID].rearrange("p (h d) -> p h d", d=D),
                                     ACT.Copy).then_inc(s["v1"], 1)
                weights(n, 0)
                weights(n, 1)
                if front:
                    head_roots(n + 1)
                query_features(n, 0)
                if not front:
                    modulate2(0, 0, c0)
                query_features(n, 1)
                if not front:
                    modulate2(0, 1, c0)
                weights_hi(n, 0)
                weights_hi(n, 1)

            def weight_hi(i):
                act.wait_ge(ld_ffn[i], 16 * len(raw_ffn[i]))
                w = FFN * KT // len(raw_ffn[i])
                for j, part in enumerate(raw_ffn[i]):
                    a = nc.scalar.activation(wf_hi[:, i, j * w:(j + 1) * w], part, ACT.Copy)
                a.then_inc(fb["wfh"], 1)

            def gate_size(j):
                act.wait_ge(pr["gates"], j + 1)
                src = big[1][:, :] if j == 0 else acc[:, :, :].rearrange("p a n -> p (a n)")
                nc.scalar.activation(gates[:, j, :, :].rearrange("p b n -> p (b n)"), src, ACT.Abs).then_inc(pr["gabs"], 1)

            roots(1, 0, TPB)
            act.wait_ge(pr["wqk"], 1)
            nc.scalar.activation(wqk_hi[:, :, :].rearrange("p k n -> p (k n)"), big[1][:, :], ACT.Copy).then_inc(pr["wqkhi"], 1)
            act.wait_ge(ld_vo, 32)
            nc.scalar.activation(wvo_hi[:, :, :, :], w_in[:, 2:4, :, :], ACT.Copy).then_inc(pr["wvohi"], 1)
            act.wait_ge(pr["modt"], 2)
            modulate(0)
            head_squares(0)
            head_roots(0)
            weight_hi(0)
            gate_size(0)
            weight_hi(1)
            roots(2, TPB, TILES)
            gate_size(1)
            weight_hi(2)
            for n in range(4):
                step(n, n % 2, True, n > 0, n > 1)
            with act.Fori(2, TILES // 2 - 1) as u:
                step(u * 2, 0, True, True, True)
                step(u * 2 + 1, 1, True, True, True)
            step(TILES - 2, 0, True, True, True)
            step(TILES - 1, 1, False, True, True)
            act.preload_act_table(ACT.Silu)
            o_hi(TILES - 2)
            act.wait_ge(s["fql0"], TILES)
            silu(0, 0)
            silu(0, 1)
            o_hi(TILES - 1)
            silu(0, 2)
            silu(0, 3)
            modulate2(1, 0, c0)
            modulate2(1, 1, c1)
            silu(0, 4)
            act.preload_act_table(ACT.Sqrt)
            roots(4, TILES - ST, TILES)
            act.preload_act_table(ACT.Silu)
            for m in range(5, MT):
                silu(0, m)
            with act.Fori(0, SUPERS // 2 - 1) as u:
                super_tile(u * 2 + 1, False)
                super_tile(u * 2 + 2, False)
            super_tile(SUPERS - 1, True)

        @block.vector
        def _(dve):
            tt, ts, cp = nc.vector.tensor_tensor, nc.vector.tensor_scalar, nc.vector.tensor_copy
            nc.vector.memset(vp[:, :, :, :, :], 0.0).then_inc(pr["vp0"], 1)
            nc.vector.memset(bias_rows[:, :], 0.0).then_inc(pr["rows0"], 1)
            nc.vector.memset(bias_sel[:, :], 0.0).then_inc(pr["sel0"], 1)
            nc.vector.memset(keep[:, :], 1.0).then_inc(pr["keep0"], 1)
            nc.vector.memset(state[:, :, :], 0.0).then_inc(s["state"], 1)
            dve.wait_ge(pr["keep0"], 1)
            nc.vector.memset(vp[:, :, :, 0, D:DV], 1.0).then_inc(pr["vp"], 1)
            for r in range(3):
                a = nc.vector.memset(bias_sel[32 * r:32 * r + 1, :], 1.0)
            a.then_inc(pr["sel"], 1)
            nc.vector.memset(keep[:, 0:TILES:TPB], 0.0).then_inc(pr["keep"], 1)
            nc.vector.memset(fk_hi[:, :, NF:P], 0.0)
            nc.vector.memset(fk_lo[:, :, NF:P], 0.0).then_inc(pr["fkpad"], 1)
            dve.wait_ge(ld_small, 80)
            ts(gu, helmert, gam[:, 0:1], None, ALU.mult).then_inc(pr["gu"], 1)
            ts(bet_bc, ident, 0.0, bet[:, 0:1], ALU.mult, ALU.add).then_inc(pr["betbc"], 1)
            dve.wait_ge(pr["bias"], 1)
            b_full = acc[:, 0, 0:P]
            cp(bias_p[:, 0, :], b_full).then_inc(pr["bp1"], 1)
            dve.wait_ge(pr["bp1"], 1)
            tt(bias_r, b_full, bias_p[:, 0, :], ALU.subtract).then_inc(pr["br1"], 1)
            dve.wait_ge(pr["br1"], 1)
            cp(bias_p[:, 1, :], bias_r).then_inc(pr["bp2"], 1)
            dve.wait_ge(pr["bp2"], 1)
            tt(bias_p[:, 2, :], bias_r, bias_p[:, 1, :], ALU.subtract).then_inc(pr["bp3"], 1)
            dve.wait_ge(pr["bp3"], 1)
            for r in range(3):
                cp(bias_rows[32 * r:32 * r + 1, :].rearrange("p (g n) -> p g n", g=4),
                   bias_p[32 * r:32 * r + 1, r, :].unsqueeze(1).broadcast_to([1, 4, P])).then_inc(pr["rows"], 1)
            dve.wait_ge(pr["siluc"], 1)
            cp(silu_cb[:, :, :, :], silu_c[:, :, :].unsqueeze(3).broadcast_to([P, KT, BATCH, P])).then_inc(pr["silucb"], 1)

            def stats(first, last):
                for t in range(first, last):
                    nc.vector.bn_stats(bn[:, t, :], xs[:, t, :]).then_inc(pr["bn"], 1)

            def modulation_rows(first, last):
                dve.wait_ge(pr["mods"], last // 2)
                for j in range(first, last):
                    src = big[0][:, j * KT * BATCH:(j + 1) * KT * BATCH].rearrange("p (k b) -> p k b", k=KT)
                    for k in range(KT):
                        a = ts(modt[:, j, k, :].rearrange("p (b t) -> p b t", b=BATCH),
                               src[:, k, :].unsqueeze(2).broadcast_to([P, BATCH, TPB]), 1.0 if j % 2 == 0 else 0.0, None,
                               ALU.add)
                    a.then_inc(pr["modt"], 1)

            def norms(time, first, last):
                m_e, v_e, m_o, v_o = (bn[:, first:last, i] for i in (1, 2, 4, 5))
                a, b, d, mu, r = (x[:, first:last] for x in (na, nb, nd, mean, rstd))
                tt(d, m_e, m_o, ALU.add).then_inc(nr["m"], 1)
                dve.wait_ge(nr["m"], time)
                ts(mu, d, 0.5, None, ALU.mult).then_inc(nr["mean"], 1)
                tt(a, v_e, v_o, ALU.add).then_inc(nr["v"], 1)
                dve.wait_ge(nr["mean"], time)
                tt(d, m_e, m_o, ALU.subtract).then_inc(nr["d"], 1)
                dve.wait_ge(nr["d"], time)
                nc.vector.scalar_tensor_tensor(r, d, 0.25, d, ALU.mult, ALU.mult).then_inc(nr["d2"], 1)
                dve.wait_ge(nr["v"], time)
                dve.wait_ge(nr["d2"], time)
                nc.vector.scalar_tensor_tensor(d, a, 1.0 / HID, r, ALU.mult, ALU.add).then_inc(nr["a"], 1)
                dve.wait_ge(nr["a"], time)
                ts(a, d, LN_EPS, None, ALU.add).then_inc(nr["ae"], 1)
                dve.wait_ge(nr["s"], time)
                nc.vector.reciprocal(d, b).then_inc(nr["y"], 1)
                dve.wait_ge(nr["y"], time)
                nc.vector.scalar_tensor_tensor(b, d, -0.5, d, ALU.mult, ALU.mult).then_inc(nr["t"], 1)
                dve.wait_ge(nr["t"], time)
                tt(r, b, a, ALU.mult).then_inc(nr["u"], 1)
                dve.wait_ge(nr["u"], time)
                nc.vector.scalar_tensor_tensor(r, r, 1.5, d, ALU.add, ALU.mult).then_inc(nr["r"], 1)
                dve.wait_ge(nr["r"], time)

            def row(n):
                return xs[:, bass.ds(n, 1), :].rearrange("p a d -> p (a d)")

            def layer_norm(n):
                wait(dve, s["xT"], n)
                ts(xn[:, :], row(n), mean[:, bass.ds(n, 1)], rstd[:, bass.ds(n, 1)],
                   ALU.subtract, ALU.mult).then_inc(s["xn"], 1)

            def split_h(n, b):
                dve.wait_ge(s["hT"], n + 1)
                wait(dve, s["v"], n - 1)
                cp(h_hi[:, b, :, :], hT[:, :, :]).then_inc(s["h_hi"], 1)
                dve.wait_ge(s["h_hi"], n + 1)
                tt(h_lo[:, b, :, :], hT[:, :, :], h_hi[:, b, :, :].bitcast(F32), ALU.subtract).then_inc(s["h_split"], 1)

            def head_sums(n):
                dve.wait_ge(s["sq"], n + 1)
                nc.vector.tensor_reduce(rt[:, :], sq[:, :, :], axis=AX.X, op=ALU.add).then_inc(s["ss"], 1)
                dve.wait_ge(s["ss"], n + 1)
                ts(ra[:, :], rt[:, :], 1.0 / D, LN_EPS, ALU.mult, ALU.add).then_inc(s["ra"], 1)

            def head_norms(n, ms_of=None, b=0):
                part = [ms[:, b, i, :, :].rearrange("p h d -> p (h d)") for i in range(PARTS)]
                rest = ms_r[:, :, :].rearrange("p h d -> p (h d)")
                m = ms_of
                if n is not None:
                    dve.wait_ge(s["rs"], n + 1)
                    nc.vector.reciprocal(ry[:, :], rs[:, :]).then_inc(s["ry0"], 1)
                if m is not None:
                    dve.wait_ge(s["msp"], m + 1)
                    wait(dve, s["accp1"], m - 1)
                    ts(part[0], c2[:, 0:HEADS * DV], keep[:, bass.ds(m, 1)], None, ALU.mult).then_inc(s["ms1"], 1)
                if n is not None:
                    dve.wait_ge(s["ry0"], n + 1)
                    nc.vector.scalar_tensor_tensor(rt[:, :], ry[:, :], -0.5, ry[:, :], ALU.mult,
                                                   ALU.mult).then_inc(s["rt0"], 1)
                if m is not None:
                    dve.wait_ge(s["ms1"], m + 1)
                    dve.wait_ge(s["v3"], m + 1)
                    nc.vector.scalar_tensor_tensor(rest, c2[:, 0:HEADS * DV], keep[:, bass.ds(m, 1)], part[0],
                                                   ALU.mult, ALU.subtract).then_inc(s["msr"], 1)
                if n is not None:
                    dve.wait_ge(s["rt0"], n + 1)
                    tt(rt[:, :], rt[:, :], ra[:, :], ALU.mult).then_inc(s["rt1"], 1)
                if m is not None:
                    dve.wait_ge(s["msr"], m + 1)
                    cp(part[1], rest).then_inc(s["ms2"], 1)
                if n is not None:
                    dve.wait_ge(s["rt1"], n + 1)
                    nc.vector.scalar_tensor_tensor(rt[:, :], rt[:, :], 1.5, ry[:, :], ALU.add, ALU.mult).then_inc(s["ry"], 1)
                if m is not None:
                    dve.wait_ge(s["ms2"], m + 1)
                    tt(part[2], rest, part[1], ALU.subtract).then_inc(s["ms3"], 1)
                if n is not None:
                    dve.wait_ge(s["ry"], n + 1)
                    tt(qn[:, :, :], c0[:, :].rearrange("p (h d) -> p h d", d=D),
                       rt[:, :].unsqueeze(2).broadcast_to([P, 2 * HEADS, D]), ALU.mult).then_inc(s["qn"], 1)
                    dve.wait_ge(s["qn"], n + 1)
                    wait(dve, s["qTp"], n)
                    wait(dve, s["kTp"], n)
                    cp(k16[:, :, 0:4:2, :], qn[:, HEADS:, :].unsqueeze(2).broadcast_to([P, HEADS, 2, D])).then_inc(s["k_hi"], 1)
                    cp(q16[:, :, 0:2, :], qn[:, 0:HEADS, :].unsqueeze(2).broadcast_to([P, HEADS, 2, D])).then_inc(s["q_hi"], 1)
                    dve.wait_ge(s["q_hi"], n + 1)
                    tt(q16[:, :, 2:4, :], qn[:, 0:HEADS, :].unsqueeze(2).broadcast_to([P, HEADS, 2, D]),
                       q16[:, :, 0:2, :], ALU.subtract).then_inc(s["q_lo"], 1)

            def split_v(n, b):
                dve.wait_ge(s["v1"], n + 1)
                wait(dve, s["ms3"], n)
                tt(v_r1, c2[:, 0:HID].rearrange("p (h d) -> p h d", d=D), vp[:, b, :, 0, 0:D],
                   ALU.subtract).then_inc(s["vr1"], 1)
                dve.wait_ge(s["vr1"], n + 1)
                cp(vp[:, b, :, 1, 0:D], v_r1).then_inc(s["v2"], 1)

            def update_state(n):
                dve.wait_ge(s["sdp1"], n + 1)
                nc.vector.scalar_tensor_tensor(state[:, :, :].rearrange("p h d -> p (h d)"),
                                               state[:, :, :].rearrange("p h d -> p (h d)"), keep[:, bass.ds(n, 1)],
                                               c2[:, 0:HEADS * DV], ALU.mult, ALU.add).then_inc(s["state"], 1)

            def normalize(n):
                dve.wait_ge(s["intra1"], n + 1)
                ts(den[:, :], acc_h[:, :, D], D * ATT_EPS, None, ALU.add).then_inc(s["den"], 1)
                dve.wait_ge(s["den"], n + 1)
                nc.vector.reciprocal(rden[:, :], den[:, :]).then_inc(s["rden"], 1)
                dve.wait_ge(s["rden"], n + 1)
                tt(o_n[:, :, :], acc_h[:, :, 0:D], rden[:, :].unsqueeze(2).broadcast_to([P, HEADS, D]),
                   ALU.mult).then_inc(s["o_n"], 1)

            def o_lo(n):
                dve.wait_ge(s["oT_hi"], n + 1)
                tt(oT_lo[:, :, :].rearrange("p k n -> p (k n)"), c2[:, 0:HID],
                   oT_hi[:, :, :].rearrange("p k n -> p (k n)").bitcast(F32), ALU.subtract).then_inc(s["oT_lo"], 1)

            def gate_y(n):
                dve.wait_ge(s["y"], n + 1)
                wait(dve, s["x1"], n)
                if isinstance(n, int) and n == 0:
                    dve.wait_ge(pr["gfin"], 2)
                tt(yg[:, :], c1[:, 0:HID], gates[:, 0, bass.ds(n // TPB, 1), :].rearrange("p a d -> p (a d)"),
                   ALU.mult).then_inc(s["yg"], 1)

            def stats2(n):
                dve.wait_ge(s["x1"], n + 1)
                nc.vector.bn_stats(bn[:, bass.ds(n, 1), :].rearrange("p a d -> p (a d)"), row(n)).then_inc(s["bn2"], 1)

            def low(name, n, i, w=P):
                full, hi, lo = {"fk": (fk, fk_hi, fk_lo), "at": (at, at_hi, at_lo), "fq": (fq, fq_hi, fq_lo)}[name]
                hs = slice(i * HALF, (i + 1) * HALF)
                dve.wait_ge(s[f"{name}h{i}"], n + 1)
                tt(lo[:, hs, 0:w], full[:, hs, 0:w], hi[:, hs, 0:w], ALU.subtract).then_inc(s[f"{name}l{i}"], 1)

            def layer_norm2(t):
                wait(dve, fb["hTp"], t * 2)
                for i in range(ST):
                    a = ts(xn2[:, i, :], row(t * ST + i), mean[:, bass.ds(t * ST + i, 1)],
                           rstd[:, bass.ds(t * ST + i, 1)], ALU.subtract, ALU.mult)
                a.then_inc(fb["xn2"], 1)

            def split_h2(t, buf):
                dve.wait_ge(fb["h2"], t * 2 + 2)
                cp(h2_hi[buf], h2[:, :, :]).then_inc(fb["h2hi"], 1)
                dve.wait_ge(fb["h2hi"], t + 1)
                tt(h2_lo[buf], h2[:, :, :], h2_hi[buf].bitcast(F32), ALU.subtract).then_inc(fb["h2lo"], 1)

            def finish(t):
                dve.wait_ge(fb["down"], t + 1)
                wait(dve, fb["ob"], t)
                for i in range(ST):
                    a = tt(yb[:, i, :], acc[:, i // 2, (i % 2) * HID:(i % 2 + 1) * HID],
                           gates[:, 1, bass.ds(t // (TPB // ST), 1), :].rearrange("p a d -> p (a d)"), ALU.mult)
                a.then_inc(fb["yb"], 1)

            def gated(t, m):
                i = m % 2
                dve.wait_ge(fb["sg"], t * MT + m + 1)
                dve.wait_ge(fb["up"], t * MT + m + 1)
                tt(g[:, i, :], big[i][:, 512:1024], sg[:, i, :], ALU.mult).then_inc(fb["g"], 1)
                dve.wait_ge(fb["g"], t * MT + m + 1)
                cp(g_hi[:, i, :], g[:, i, :]).then_inc(fb["ghi"], 1)
                dve.wait_ge(fb["ghi"], t * MT + m + 1)
                tt(g_lo[:, i, :], g[:, i, :], g_hi[:, i, :].bitcast(F32), ALU.subtract).then_inc(fb["glo"], 1)

            def super_tile(t, buf, last):
                for m in range(MT):
                    gated(t, m)
                    if m == 0:
                        finish(t - 1)
                    if m == 1 and not last:
                        layer_norm2(t + 1)
                    if m == 4 and not last:
                        split_h2(t + 1, 1 - buf)

            def gate_values(j):
                dve.wait_ge(pr["g1"], 1)
                dve.wait_ge(pr["g2"], 1)
                g_j = gates[:, j, :, :].rearrange("p b n -> p (b n)")
                nc.vector.scalar_tensor_tensor(g_j, sign[:, j * BATCH * HID:(j + 1) * BATCH * HID], -1.0, g_j,
                                               ALU.add, ALU.mult).then_inc(pr["gfin"], 1)

            def step(n, b, front, back, back2):
                dve.wait_ge(s["qTp"], n + 1)
                cp(qT[:, :, :].rearrange("p j n -> p (j n)"), c0[:, :].bitcast(F16)).then_inc(s["qT"], 1)
                if back:
                    update_state(n - 1)
                    low("at", n - 1, 0)
                if isinstance(n, int) and n == 0:
                    gate_values(0)
                if front:
                    split_h(n + 1, 1 - b)
                if isinstance(n, int) and n == 0:
                    gate_values(1)
                if back:
                    low("at", n - 1, 1)
                if back2:
                    o_lo(n - 2)
                if not isinstance(n, int) or n > 2:
                    stats2(n - 3)
                if not front:
                    norms(3, 0, TILES - ST)
                if front:
                    low("fk", n, 0, NF)
                if front:
                    head_sums(n + 1)
                split_v(n, b)
                if not front:
                    layer_norm2(0)
                else:
                    low("fk", n, 1, NF)
                head_norms(n + 1 if front else None, n, b)
                if not front:
                    split_h2(0, 1)
                if back2:
                    gate_y(n - 2)
                if front and not (isinstance(n, int) and n == TILES - 2):
                    layer_norm(n + 2)
                if back:
                    normalize(n - 1)

            dve.wait_ge(pr["vp"], 1)
            dve.wait_ge(pr["fkpad"], 1)
            dve.wait_ge(pr["keep"], 1)
            dve.wait_ge(ld_x[0], 16)
            stats(0, TPB)
            modulation_rows(0, 2)
            dve.wait_ge(pr["bn"], TPB)
            norms(1, 0, TPB)
            layer_norm(0)
            dve.wait_ge(pr["wqkhi"], 1)
            tt(wqk_lo[:, :, :].rearrange("p k n -> p (k n)"), big[1][:, :],
               wqk_hi[:, :, :].rearrange("p k n -> p (k n)").bitcast(F32), ALU.subtract).then_inc(pr["wqklo"], 1)
            split_h(0, 0)
            dve.wait_ge(pr["wvohi"], 1)
            tt(wvo_lo[:, :, :, :], w_in[:, 2:4, :, :], wvo_hi[:, :, :, :].bitcast(F32), ALU.subtract).then_inc(pr["wvolo"], 1)
            dve.wait_ge(ld_x[1], 16)
            stats(TPB, 2 * TPB)
            head_sums(0)
            head_norms(0)
            layer_norm(1)
            for b in (2, 3):
                dve.wait_ge(ld_x[b], 16)
                stats(b * TPB, (b + 1) * TPB)
            modulation_rows(2, 4)
            dve.wait_ge(pr["bn"], TILES)
            norms(2, TPB, TILES)
            for j in range(2):
                dve.wait_ge(pr["gabs"], j + 1)
                src = big[1][:, :] if j == 0 else acc[:, :, :].rearrange("p a n -> p (a n)")
                a = ts(sign[:, j * BATCH * HID:(j + 1) * BATCH * HID], src, 0.0, 2.0, ALU.is_ge, ALU.mult)
            a.then_inc(pr["g1"], 1)

            flat_gates = gates[:, :, :, :].rearrange("p j b n -> p (j b n)")
            ts(flat_gates, flat_gates, 0.25, None, ALU.max).then_inc(pr["g2"], 1)
            for n in range(4):
                step(n, n % 2, True, n > 0, n > 1)
            with dve.Fori(2, TILES // 2 - 1) as u:
                step(u * 2, 0, True, True, True)
                step(u * 2 + 1, 1, True, True, True)
            step(TILES - 2, 0, True, True, True)
            step(TILES - 1, 1, False, True, True)
            low("at", TILES - 1, 0)
            low("at", TILES - 1, 1)
            o_lo(TILES - 2)
            dve.wait_ge(s["fql1"], TILES)
            gate_y(TILES - 2)
            stats2(TILES - 3)
            gated(0, 0)
            stats2(TILES - 2)
            gated(0, 1)
            normalize(TILES - 1)
            o_lo(TILES - 1)
            layer_norm2(1)
            gate_y(TILES - 1)
            dve.wait_ge(fb["down0"], 1)
            gated(0, 2)
            stats2(TILES - 1)
            gated(0, 3)
            gated(0, 4)
            split_h2(1, 0)
            norms(4, TILES - ST, TILES)
            for m in range(5, MT):
                gated(0, m)
            with dve.Fori(0, SUPERS // 2 - 1) as u:
                super_tile(u * 2 + 1, 0, False)
                super_tile(u * 2 + 2, 1, False)
            super_tile(SUPERS - 1, 0, True)
            t = (SUPERS - 1) * ST
            dve.wait_ge(fb["down"], SUPERS)
            dve.wait_ge(fb["ob"], SUPERS - 1)
            for i in range(ST):
                tt(yb[:, i, :], acc[:, i // 2, (i % 2) * HID:(i % 2 + 1) * HID], gates[:, 1, BATCH - 1, :],
                   ALU.mult).then_inc(fb["yb_last"], 1)
            dve.wait_ge(fb["yb_last"], ST)
            dve.wait_ge(fb["ob_last"], 1)
            dve.wait_ge(fb["stored"], 16 * (SUPERS - 1))
            tt(ob[:, 2:4, :], xs[:, t + 2:t + 4, :], yb[:, 2:4, :], ALU.add).then_inc(fb["ob_last"], 1)

        @block.gpsimd
        def _(pool):
            nc.gpsimd.memset(tick[:, :], 0.0).then_inc(pr["tick"], 1)
            pool.wait_ge(pr["tick"], 1)

            def low_parts(n):
                pool.wait_ge(s["k_hi"], n + 1)
                nc.gpsimd.tensor_tensor(k16[:, :, 1:4:2, :], qn[:, HEADS:, :].unsqueeze(2).broadcast_to([P, HEADS, 2, D]),
                                        k16[:, :, 0:4:2, :], ALU.subtract).then_inc(s["k_lo"], 1)

            def mask(n):
                for i in range(2):
                    a = at[:, i * HALF:(i + 1) * HALF, :]
                    pool.wait_ge(s[f"at{i}"], n + 1)
                    nc.gpsimd.tensor_tensor(tick[:, 2 + i:3 + i], tick[:, 0:1], tick[:, 1:2], ALU.add).then_inc(pr["tick"], 1)
                    nc.gpsimd.affine_select(out=a, in_=a, pattern=[[0, HALF], [1, P]], compare_op=ALU.is_ge, fill=0.0,
                                            base=0, channel_multiplier=-1).then_inc(s[f"am{i}"], 1)

            def residual(n):
                pool.wait_ge(s["yg"], n + 1)
                x1 = xs[:, bass.ds(n, 1), :].rearrange("p a d -> p (a d)")
                nc.gpsimd.tensor_tensor(x1, x1, yg[:, :], ALU.add).then_inc(s["x1"], 1)

            def third_v(n, b):
                pool.wait_ge(s["v2"], n + 1)
                nc.gpsimd.tensor_tensor(vp[:, b, :, 2, 0:D], v_r1, vp[:, b, :, 1, 0:D], ALU.subtract).then_inc(s["v3"], 1)

            def low_fq(n, i):
                pool.wait_ge(s[f"fqh{i}"], n + 1)
                hs = slice(i * HALF, (i + 1) * HALF)
                nc.gpsimd.tensor_tensor(fq_lo[:, hs, :], fq[:, hs, :], fq_hi[:, hs, :], ALU.subtract).then_inc(s[f"fql{i}"], 1)

            def step(n, b, front, back, back2):
                third_v(n, b)
                mask(n)
                if front:
                    low_parts(n + 1)
                    if back2:
                        residual(n - 2)
                low_fq(n, 0)
                low_fq(n, 1)
                if not front:
                    residual(n - 2)

            low_parts(0)
            for i in range(3):
                pool.wait_ge(fb["wfh"], i + 1)
                w = FFN * KT // len(raw_ffn[i])
                for j, part in enumerate(raw_ffn[i]):
                    a = nc.gpsimd.tensor_tensor(wf_lo[:, i, j * w:(j + 1) * w], part,
                                                wf_hi[:, i, j * w:(j + 1) * w].bitcast(F32), ALU.subtract)
                a.then_inc(fb["wfl"], 1)
            for n in range(4):
                step(n, n % 2, True, n > 0, n > 1)
            with pool.Fori(2, TILES // 2 - 1) as u:
                step(u * 2, 0, True, True, True)
                step(u * 2 + 1, 1, True, True, True)
            step(TILES - 2, 0, True, True, True)
            step(TILES - 1, 1, False, True, True)
            residual(TILES - 2)
            residual(TILES - 1)

            def finish(t):
                pool.wait_ge(fb["yb"], t + 1)
                wait(pool, fb["stored"], t * 16)
                nc.gpsimd.tensor_tensor(ob[:, :, :], xs[:, bass.ds(t * ST, ST), :], yb[:, :, :], ALU.add).then_inc(fb["ob"], 1)

            finish(0)
            with pool.Fori(1, SUPERS - 1) as t:
                finish(t)
            t = (SUPERS - 1) * ST
            pool.wait_ge(fb["yb_last"], 2)
            pool.wait_ge(fb["stored"], 16 * (SUPERS - 1))
            nc.gpsimd.tensor_tensor(ob[:, 0:2, :], xs[:, t:t + 2, :], yb[:, 0:2, :], ALU.add).then_inc(fb["ob_last"], 1)


def kernel(L0_attn_hidden_states, L0_attn_Wq, L0_attn_Wk, L0_attn_Wv, L0_attn_Wo, L0_attn_gamma, L0_attn_beta,
           L0_ffn_w_gate, L0_ffn_w_up, L0_ffn_w_down, L0_c, L0_wmod):
    import numpy as _np
    import concourse.bacc as _bacc
    from concourse.bass_utils import run_bass_kernel_spmd as _run

    const32, const16 = shape_constants()
    arrays = {
        "in_x": _np.asarray(L0_attn_hidden_states).reshape(BATCH * SEQ, HID),
        "in_wq": _np.asarray(L0_attn_Wq),
        "in_wk": _np.asarray(L0_attn_Wk),
        "in_wv_t": _np.asarray(L0_attn_Wv).T,
        "in_wo_t": _np.asarray(L0_attn_Wo).T,
        "in_gamma": _np.tile(_np.asarray(L0_attn_gamma), P // D).reshape(P, 1),
        "in_beta": _np.tile(_np.asarray(L0_attn_beta), P // D).reshape(P, 1),
        "in_wg_t": _np.asarray(L0_ffn_w_gate).T,
        "in_wu_t": _np.asarray(L0_ffn_w_up).T,
        "in_wd_t": _np.asarray(L0_ffn_w_down).T,
        "in_c_t": _np.asarray(L0_c).T,
        "in_wmod": _np.asarray(L0_wmod),
        "const32": const32,
        "const16": const16,
    }
    arrays = {k: _np.ascontiguousarray(a) for k, a in arrays.items()}
    nc = _bacc.Bacc("TRN2", target_bir_lowering=False, num_devices=1)
    args = [nc.dram_tensor(k, a.shape, mybir.dt.from_np(a.dtype), kind="ExternalInput").ap() for k, a in arrays.items()]
    out = nc.dram_tensor("out", (BATCH * SEQ, HID), mybir.dt.float32, kind="ExternalOutput").ap()
    build(nc, *args, out)
    r = _run(nc, [arrays], core_ids=[0])
    return r.results[0]["out"].reshape(BATCH, SEQ, HID)
```
